# Optimizing a Trainium2 kernel written in Bass

```python
import numpy as np
import jax
import jax.numpy as jnp

def _softmax(x, axis=-1):
    return jax.nn.softmax(x, axis=axis)

def _gelu(x):
    return jax.nn.gelu(x, approximate=True)

def _silu(x):
    return jax.nn.silu(x)

def _sigmoid(x):
    return jax.nn.sigmoid(x)

def _layernorm(x, axis=-1, eps=1e-05):
    m = jnp.mean(x, axis=axis, keepdims=True)
    v = jnp.var(x, axis=axis, keepdims=True)
    return (x - m) / jnp.sqrt(v + eps)

def _scatter_add(tgt, idx, src, axis=0):
    return tgt.at[idx].add(src)

def _segment_sum(src, seg, n):
    return jax.ops.segment_sum(src, seg, n)
kernel_name = 'mk_xattn_ffn_d1_seqx_r8_828e6c'

def setup_inputs(seed: int=0):
    np.random.seed(seed)
    _w = jnp.asarray

    def _rec_inputs():
        import jax
        import jax.numpy as jnp
        _rk = jax.random.key(seed)
        x = 7.22e-05 + 1 * jax.random.normal(jax.random.fold_in(_rk, 1), (64, 128, 128), jnp.float32)
        _lenS = 128 - jax.random.randint(jax.random.fold_in(_rk, 7), (64,), 0, max(1, 128 // 4) + 1, jnp.int32)
        _lenS2 = 77 - jax.random.randint(jax.random.fold_in(_rk, 8), (64,), 0, max(1, 77 // 4) + 1, jnp.int32)
        _ctx_768P = jax.random.normal(jax.random.fold_in(_rk, 11), (64, 16, 96), jnp.float32)
        _ctx_768c = jax.random.dirichlet(jax.random.fold_in(_rk, 511), 0.3 * jnp.ones((16,), jnp.float32), (64, 77))
        _ctx_768t = jnp.einsum('bsk,bkd->bsd', _ctx_768c, _ctx_768P)
        _ctx_768t = _ctx_768t * jax.lax.rsqrt(jnp.mean(jnp.square(_ctx_768t)) + 1e-12) * 0.953939
        ctx_768 = 2.09791e-05 + 1.00001 * (_ctx_768t + 0.3 * jax.random.normal(jax.random.fold_in(_rk, 611), (64, 77, 96), jnp.float32))
        return (x, ctx_768)
    x, ctx_768 = _rec_inputs()

    def _L0_xattn_setup():
        import jax, jax.numpy as jnp
        import numpy as np
        NUM_HEADS = 16
        key = jax.random.key(seed)
        ks = jax.random.split(key, 8)
        dim, cond_dim = (128, 96)
        B, N, condN = (4, 256, 128)
        s = lambda k, shp, fan: jax.random.normal(k, shp, dtype=jnp.float32) * fan ** (-0.5)
        return {'x': jax.random.normal(ks[0], (B, N, dim), dtype=jnp.float32), 'cond': jax.random.normal(ks[1], (B, condN, cond_dim), dtype=jnp.float32), 'q_w': s(ks[2], (dim, dim), dim), 'q_b': jnp.zeros((dim,), jnp.float32), 'kv_w': s(ks[3], (cond_dim, 2 * dim), cond_dim), 'kv_b': jnp.zeros((2 * dim,), jnp.float32), 'proj_w': s(ks[4], (dim, dim), dim), 'proj_b': jnp.zeros((dim,), jnp.float32)}
    _L0_xattn_all = _L0_xattn_setup()
    _L0_xattn_in = {k: v for k, v in _L0_xattn_all.items() if k in ('q_w', 'q_b', 'kv_w', 'kv_b', 'proj_w', 'proj_b')}
    del _L0_xattn_all

    def _L0_ffn_setup():
        import jax, jax.numpy as jnp
        import numpy as np
        E = 8
        K = 2
        D = 128
        H = 4 * D
        EPS = 1e-05
        TEMP = 1.5
        key = jax.random.key(seed)
        ks = jax.random.split(key, 6)
        B, T = (2, 256)
        x = jax.random.normal(ks[0], (B, T, D), dtype=jnp.float32)
        gamma = jnp.ones((D,), dtype=jnp.float32)
        beta = jnp.zeros((D,), dtype=jnp.float32)
        router_w = jax.random.normal(ks[1], (E, D), dtype=jnp.float32) * 0.02
        W1 = jax.random.normal(ks[2], (E, D, H), dtype=jnp.float32) * 0.02
        W2 = jax.random.normal(ks[3], (E, H, D), dtype=jnp.float32) * 0.02
        return {'x': x, 'gamma': gamma, 'beta': beta, 'router_w': router_w, 'W1': W1, 'W2': W2}
    _L0_ffn_all = _L0_ffn_setup()
    _L0_ffn_in = {k: v for k, v in _L0_ffn_all.items() if k in ('gamma', 'beta', 'router_w', 'W1', 'W2')}
    del _L0_ffn_all
    return {'x': x, 'ctx_768': ctx_768, 'L0_xattn_q_w': _L0_xattn_in['q_w'], 'L0_xattn_q_b': _L0_xattn_in['q_b'], 'L0_xattn_kv_w': _L0_xattn_in['kv_w'], 'L0_xattn_kv_b': _L0_xattn_in['kv_b'], 'L0_xattn_proj_w': _L0_xattn_in['proj_w'], 'L0_xattn_proj_b': _L0_xattn_in['proj_b'], 'L0_ffn_gamma': _L0_ffn_in['gamma'], 'L0_ffn_beta': _L0_ffn_in['beta'], 'L0_ffn_router_w': _L0_ffn_in['router_w'], 'L0_ffn_W1': _L0_ffn_in['W1'], 'L0_ffn_W2': _L0_ffn_in['W2']}

def reference(x, ctx_768, L0_xattn_q_w, L0_xattn_q_b, L0_xattn_kv_w, L0_xattn_kv_b, L0_xattn_proj_w, L0_xattn_proj_b, L0_ffn_gamma, L0_ffn_beta, L0_ffn_router_w, L0_ffn_W1, L0_ffn_W2):
    import jax
    import jax.numpy as jnp

    def _L0_xattn_ref(x, cond, q_w, q_b, kv_w, kv_b, proj_w, proj_b):
        import jax, jax.numpy as jnp
        import numpy as np
        NUM_HEADS = 16
        B, N, C = x.shape
        condN = cond.shape[1]
        H = NUM_HEADS
        hd = C // H
        scale = hd ** (-0.5)
        q = (x @ q_w + q_b).reshape(B, N, H, hd).transpose(0, 2, 1, 3)
        kv = (cond @ kv_w + kv_b).reshape(B, condN, 2, H, hd)
        k = kv[:, :, 0].transpose(0, 2, 1, 3)
        v = kv[:, :, 1].transpose(0, 2, 1, 3)
        attn = jnp.einsum('bhnd,bhmd->bhnm', q * scale, k)
        attn = jax.nn.softmax(attn, axis=-1)
        out = jnp.einsum('bhnm,bhmd->bhnd', attn, v)
        out = out.transpose(0, 2, 1, 3).reshape(B, N, C)
        return out @ proj_w + proj_b

    def _L0_ffn_ref(x, gamma, beta, router_w, W1, W2):
        import jax, jax.numpy as jnp
        import numpy as np
        E = 8
        K = 2
        D = 128
        H = 4 * D
        EPS = 1e-05
        TEMP = 1.5
        res = x
        mu = jnp.mean(x, axis=-1, keepdims=True)
        var = jnp.mean(jnp.square(x - mu), axis=-1, keepdims=True)
        xn = (x - mu) * jax.lax.rsqrt(var + EPS) * gamma + beta
        logits = jnp.einsum('btd,ed->bte', xn, router_w)
        probs = jax.nn.softmax(logits / TEMP, axis=-1)
        w, idx = jax.lax.top_k(probs, K)
        wdense = jnp.sum(jax.nn.one_hot(idx, E, dtype=w.dtype) * w[..., None], axis=-2)
        h = jax.nn.silu(jnp.einsum('btd,edf->betf', xn, W1))
        y = jnp.einsum('betf,efd->betd', h, W2)
        out = jnp.einsum('bte,betd->btd', wdense, y)
        return out + res
    x = x + _L0_xattn_ref(_layernorm(x, axis=-1), ctx_768, L0_xattn_q_w, L0_xattn_q_b, L0_xattn_kv_w, L0_xattn_kv_b, L0_xattn_proj_w, L0_xattn_proj_b)
    x = x + _L0_ffn_ref(_layernorm(x, axis=-1), L0_ffn_gamma, L0_ffn_beta, L0_ffn_router_w, L0_ffn_W1, L0_ffn_W2)
    return x

_drawn_inputs = setup_inputs


def setup_inputs(seed=0):
    import zlib

    import numpy as np

    out = dict(_drawn_inputs(seed))
    spreads = {'L0_xattn_q_b': (0.0, 0.347),
     'L0_xattn_kv_b': (0.0, 0.1),
     'L0_xattn_proj_b': (0.0, 0.1),
     'L0_ffn_gamma': (1.0, 0.6),
     'L0_ffn_beta': (0.0, 0.8)}
    factors = {'L0_ffn_router_w': 8.0, 'L0_ffn_W1': 8.0, 'L0_ffn_W2': 8.0}
    for name, (base, spread) in spreads.items():
        noise = np.random.default_rng([zlib.crc32(name.encode()), seed]).standard_normal(out[name].shape)
        drawn = base * np.exp(spread * noise) if base else spread * noise
        out[name] = jnp.asarray(drawn.astype(out[name].dtype))
    for name, factor in factors.items():
        out[name] = (out[name] * factor).astype(out[name].dtype)
    return out
```

```python
from contextlib import ExitStack

import concourse.bass as bass
from concourse import mybir

F = mybir.dt.float32
R = mybir.dt.float32r
U32 = mybir.dt.uint32
ALU = mybir.AluOpType
ACT = mybir.ActivationFunctionType
AX = mybir.AxisListType

NB, S, D = 64, 128, 128
CS, CD = 77, 96
H, HD = 16, 8
E, FF = 8, 512
NC = NB // 4
TC = 4 * S
KC = 4 * CS
SCALE = float(HD) ** -0.5
EPS = 1e-5
TEMP = 1.5


class Queue:

    def __init__(self, sems):
        self.items, self.sems, self.seen = [], sems, {}

    def wait(self, name, value):
        if value > self.seen.get(name, 0):
            self.seen[name] = value
            self.items.append((name, value))

    def do(self, fn, sem=None, n=1):
        self.items.append((fn, sem, n))
        if sem is not None:
            self.sems.count[sem] = self.sems.count.get(sem, 0) + n

    def emit(self, eng):
        for it in self.items:
            if isinstance(it[0], str):
                eng.wait_ge(self.sems[it[0]], it[1])
            else:
                ins = it[0](eng)
                if it[1] is not None:
                    ins.then_inc(self.sems[it[1]], it[2])


class Sems:

    def __init__(self, nc, ctx):
        self.nc, self.ctx, self.count, self.made = nc, ctx, {}, {}

    def __getitem__(self, name):
        if name not in self.made:
            self.made[name] = self.ctx.enter_context(self.nc.semaphore("s_" + name))
        return self.made[name]


class Banks:

    def __init__(self, name, tiles):
        self.name, self.tiles, self.n = name, tiles, 0

    def take(self, q):
        k = self.n
        self.n += 1
        slot, use = k % len(self.tiles), k // len(self.tiles)
        q.wait(f"{self.name}{slot}", use)
        return self.tiles[slot], f"{self.name}{slot}"


class InOrder(Banks):

    def take(self, q):
        k = self.n
        self.n += 1
        q.wait(self.name, k - len(self.tiles) + 1)
        return self.tiles[k % len(self.tiles)], self.name


def xattn_moe(nc, x, ctx_in, qw, qb, kw, kb, vw, vb, pw, pb, gam, bet, rwT, W1, W2, ident, sel, one24, iota, out):
    st = ExitStack()
    with st:
        sems = Sems(nc, st)
        pe, act, dve, pool, sp = (Queue(sems) for _ in range(5))

        def sbt(ctx, name, shape, dt=F):
            return ctx.enter_context(nc.sbuf_tensor(name, shape, dt))

        xres = nc.dram_tensor("xres", (NC, 128, 512), F, kind="Internal").ap()
        wsc = nc.dram_tensor("wsc", (NC, 32, 128), F, kind="Internal").ap()

        xnT = sbt(st, "xnT", [128, NC * TC])
        idf = sbt(st, "idf", [128, 128])

        sa = ExitStack()
        nm_ = [0]

        def A(shape, dt=F, n=1):
            nm_[0] += 1
            ts = [sbt(sa, f"a{nm_[0]}_{i}", shape, dt) for i in range(n)]
            return ts[0] if n == 1 else ts

        selr = A([128, 16, 128], R)
        stg = A([128, 4, 128], F, 2)
        qwh, qwl, rwh, rwl = (A([128, 128], R) for _ in range(4))
        kwh, kwl = (A([CD, 128], R) for _ in range(2))
        vwf = A([CD, 128])
        pwf = A([128, 128])
        wst = A([128, 3, 128])
        vbb = A([CS, 128])
        pbb = A([128, 128])
        cols = A([128, 8])
        iot = A([128, 4, 8])
        nhalf = A([128, 4])
        xin = A([128, 4, 128], F, 4)
        cin = A([CS, 4, CD], F, 3)
        xh = A([128, 4, 128], F, 2)
        xTh = A([128, TC], R)
        xTl = A([128, TC], R)
        cf = A([CD, KC], F, 2)
        ch, cl = A([CD, KC], R), A([CD, KC], R)
        qf = A([128, TC])
        qh, ql = A([128, TC], R), A([128, TC], R)
        kf = A([128, KC])
        kh, kl = A([128, KC], R), A([128, KC], R)
        qc = A([128, 4, TC], R, 2)
        kc = A([128, 4, KC], R, 2)
        qd = A([128, 4, 4, S], R, 3)
        kd = A([128, 4, 4, CS], R, 3)
        v9 = A([CS, 4 * H, 9], F, 2)
        P = A([CS, 4 * S], F, 3)
        mx = A([128, 16], F, 2)
        nm = A([16, 128], R, 2)
        osb = A([128, 4, 128], F, 2)
        rd = A([128, 16], F, 2)
        on = A([128, 128], F, 2)
        oT = A([128, 128], F, 2)
        x1 = A([128, 4, 128], F, 3)
        hh = A([128, 4, 128], F, 2)
        zz = A([128, 4, 128], F, 2)
        xr = A([128, 4, 128], F, 2)
        bst = A([128, 3, 4, 6])
        mv = A([128, 3, 4, 2], F, 2)
        rs = A([128, 3, 4], F, 2)
        ve = A([128, 3, 4], F, 2)
        zh, zl = A([128, TC], R), A([128, TC], R)
        lg = A([8, TC])
        sm = A([128, 4, 4, 8], F, 2)
        s4 = A([128, 3, 4], F, 2)
        m8 = A([128, 4, 8], F, 2)
        i8 = A([128, 4, 8], U32, 2)
        if8 = A([128, 4, 8], F, 2)
        wd = A([128, 4, 8], F, 2)
        wts = A([32, 128], F, 2)

        pa = ExitStack()

        def pt(ctx, name, n):
            return [ctx.enter_context(nc.psum_tensor(f"{name}{i}", [128, 512], F)) for i in range(n)]

        misc, bS, bT = Banks("misc", pt(pa, "pm", 2)), Banks("bS", pt(pa, "ps", 2)), Banks("bT", pt(pa, "pt", 2))
        bO, bX = Banks("bO", pt(pa, "po", 1)), Banks("bX", pt(pa, "px", 1))

        def load(dst, src, sem):
            sp.do(lambda e: e.dma_start(dst, src), sem, 16)

        load(idf[:, :], ident, "ld_id")
        for t, (dst, src) in enumerate(((wst[:, 0, :], qw), (wst[0:CD, 1, :], kw), (wst[:, 2, 0:8], rwT), (vwf[:, :], vw),
                                        (pwf[:, :], pw), (vbb[:, :], vb), (pbb[:, :], pb), (cols[:, 0:1], qb),
                                        (cols[:, 1:2], kb), (cols[:, 2:3], gam), (cols[:, 3:4], bet),
                                        (cols[:, 4:5], one24), (iot[:, :, :], iota))):
            load(dst, src, "ld_w")
        n_ldw = sems.count["ld_w"]

        dve.do(lambda e: e.memset(nhalf[:, :], -0.5), "c_nh")
        for i in range(2):
            dve.do(lambda e, i=i: e.memset(v9[i][:, :, :], 1.0), "c_v9")
            dve.do(lambda e, i=i: e.memset(osb[i][:, :, :], 0.0), "c_z")
        for i in range(3):
            pool.do(lambda e, i=i: e.memset(qd[i][:, :, :, :].bitcast(F), 0.0), "c_qd")
            pool.do(lambda e, i=i: e.memset(kd[i][:, :, :, :].bitcast(F), 0.0), "c_kd")
        dve.do(lambda e: e.memset(bO.tiles[0][:, :], 0.0), "c_o")
        dve.do(lambda e: e.memset(rwh[:, :].bitcast(F), 0.0), "c_rw")
        dve.do(lambda e: e.memset(rwl[:, :].bitcast(F), 0.0), "c_rw")
        dve.wait("ld_w", n_ldw)
        dve.wait("c_rw", 2)
        dve.do(lambda e: e.tensor_scalar(cols[:, 0:1], cols[:, 0:1], SCALE, None, ALU.mult), "c_qb")
        for hi, src, k in ((qwh[:, :], wst[:, 0, :], "qw"), (kwh[:, :], wst[0:CD, 1, :], "kw"), (rwh[:, 0:8], wst[:, 2, 0:8], "rw")):
            dve.do(lambda e, hi=hi, src=src: e.tensor_copy(hi, src), "c_hi")
        dve.wait("c_hi", 3)
        for hi, lo, src in ((qwh[:, :], qwl[:, :], wst[:, 0, :]), (kwh[:, :], kwl[:, :], wst[0:CD, 1, :]),
                            (rwh[:, 0:8], rwl[:, 0:8], wst[:, 2, 0:8])):
            dve.do(lambda e, hi=hi, lo=lo, src=src: e.tensor_tensor(lo, src, hi.bitcast(F), ALU.subtract), "c_lo")
        for g in range(4):
            if g >= 2:
                sp.wait("c_sel", g - 1)
            load(stg[g % 2][:, :, :], sel[:, 4 * g:4 * g + 4, :], f"ld_sel{g % 2}")
            act.wait(f"ld_sel{g % 2}", 16 * (g // 2 + 1))
            act.do(lambda e, g=g: e.copy(selr[:, 4 * g:4 * g + 4, :], stg[g % 2][:, :, :]), "c_sel")

        done = {}

        def LX(c):
            if c >= 4:
                sp.wait(*done[("x1", 4 * (c - 4) + 3)])
            load(xin[c % 4][:, :, :], x[4 * c:4 * c + 4].rearrange("b n d -> n b d"), f"lx{c % 4}")
            if c >= 3:
                sp.wait("cT", c - 2)
            load(cin[c % 3][:, :, :], ctx_in[4 * c:4 * c + 4].rearrange("b m d -> m b d"), f"lc{c % 3}")

        def norm_stats(c, k, src):
            b = c % 2
            if c >= 1:
                dve.wait(f"mv{k}", 4 * c)
            for i in range(4):
                dve.do(lambda e, i=i: e.bn_stats(bst[:, k, i, :], src[:, i, :]), f"bst{k}")
            dve.wait(f"bst{k}", 4 * c + 4)
            if c >= 2:
                dve.wait(f"rs{k}", c - 1)
            for i in range(4):
                dve.do(lambda e, i=i: e.bn_aggr(mv[b][:, k, i, :], bst[:, k, i, :]), f"mv{k}")
            pool.wait("c_nh", 1)
            pool.wait(f"mv{k}", 4 * c + 4)
            pool.do(lambda e: e.tensor_scalar(ve[b][:, k, :], mv[b][:, k, :, 1], EPS, None, ALU.add), f"ve{k}")
            pool.wait(f"ve{k}", c + 1)
            pool.do(lambda e: e.tensor_tensor(rs[b][:, k, :], ve[b][:, k, :], nhalf[:, :], ALU.pow), f"rs{k}")

        def norm_apply(c, k, dst, src, sem):
            b = c % 2
            dve.wait(f"rs{k}", c + 1)
            for i in range(4):
                dve.do(lambda e, i=i: e.tensor_scalar(dst[:, i, :], src[:, i, :], mv[b][:, k, i, 0:1], rs[b][:, k, i:i + 1],
                                                      ALU.subtract, ALU.mult), sem)

        def LN1(c):
            dve.wait(f"lx{c % 4}", 16 * (c // 4 + 1))
            norm_stats(c, 0, xin[c % 4])

        def XH(c):
            if c >= 2:
                dve.wait("xT", c - 1)
            norm_apply(c, 0, xh[c % 2], xin[c % 4], "xh")
            pool.wait("ld_w", n_ldw)
            pool.wait("xh", 4 * c + 4)
            for i in range(4):
                pool.do(lambda e, i=i: e.tensor_tensor(xin[c % 4][:, i, :], xin[c % 4][:, i, :], pbb[:, :], ALU.add), "xp")

        def XT(c):
            pe.wait("ld_id", 16)
            pe.wait("xh", 4 * c + 4)
            t, s = misc.take(pe)
            for i in range(4):
                pe.do(lambda e, i=i: e.transpose(t[:, i * 128:(i + 1) * 128], xh[c % 2][:, i, :], idf[:, :]),
                      "xT" if i == 3 else None)
            act.wait("xT", c + 1)
            act.wait("q", c)
            act.do(lambda e: e.copy(xTh[:, :], t[:, :]), "xTh")
            dve.wait("xTh", c + 1)
            dve.do(lambda e: e.tensor_tensor(xTl[:, :], t[:, :], xTh[:, :].bitcast(F), ALU.subtract), s)
            done[("xTl", c)] = (s, sems.count[s])

        def three(pe, out, w, xs, sem):
            (wh, wl), (xh_, xl) = w, xs
            pe.do(lambda e: e.matmul(out, wl, xh_, start=True, stop=False))
            pe.do(lambda e: e.matmul(out, wh, xh_, start=False, stop=False))
            pe.do(lambda e: e.matmul(out, wh, xl, start=False, stop=True), sem)


        def QP(c):
            pe.wait("c_lo", 3)
            pe.wait(*done[("xTl", c)])
            t, s = misc.take(pe)
            three(pe, t[:, :], (qwh[:, :], qwl[:, :]), (xTh[:, :], xTl[:, :]), "q")
            act.wait("c_qb", 1)
            act.wait("q", c + 1)
            act.wait("ql", c)
            act.do(lambda e: e.activation(qf[:, :], t[:, :], ACT.Identity, bias=cols[:, 0:1], scale=SCALE), s)
            dve.wait(s, sems.count[s])
            dve.wait("qc", 4 * c)
            dve.do(lambda e: e.tensor_copy(qh[:, :], qf[:, :]), "qh")
            dve.wait("qh", c + 1)
            dve.do(lambda e: e.tensor_tensor(ql[:, :], qf[:, :], qh[:, :].bitcast(F), ALU.subtract), "ql")

        def CT(c):
            pe.wait(f"lc{c % 3}", 16 * (c // 3 + 1))
            t, s = misc.take(pe)
            for i in range(4):
                pe.do(lambda e, i=i: e.transpose(t[0:CD, i * CS:(i + 1) * CS], cin[c % 3][:, i, :], idf[0:CS, 0:CS]),
                      "cT" if i == 3 else None)
            act.wait("cT", c + 1)
            if c >= 2:
                act.wait("v", c - 1)
            act.do(lambda e: e.copy(cf[c % 2][:, :], t[0:CD, 0:KC]), s)
            dve.wait(s, sems.count[s])
            dve.wait("k", c)
            dve.do(lambda e: e.tensor_copy(ch[:, :], cf[c % 2][:, :]), "ch")
            dve.wait("ch", c + 1)
            dve.do(lambda e: e.tensor_tensor(cl[:, :], cf[c % 2][:, :], ch[:, :].bitcast(F), ALU.subtract), "cl")

        def KP(c):
            pe.wait("cl", c + 1)
            t, s = misc.take(pe)
            three(pe, t[:, 0:KC], (kwh[:, :], kwl[:, :]), (ch[:, :], cl[:, :]), "k")
            act.wait("k", c + 1)
            act.wait("kl", c)
            act.do(lambda e: e.activation(kf[:, :], t[:, 0:KC], ACT.Identity, bias=cols[:, 1:2]), s)
            dve.wait(s, sems.count[s])
            dve.wait("kc", 4 * c)
            dve.do(lambda e: e.tensor_copy(kh[:, :], kf[:, :]), "kh")
            dve.wait("kh", c + 1)
            dve.do(lambda e: e.tensor_tensor(kl[:, :], kf[:, :], kh[:, :].bitcast(F), ALU.subtract), "kl")

        def QC(c, g):
            pe.wait("c_sel", 4)
            pe.wait("ql", c + 1)
            t, s = misc.take(pe)
            pe.do(lambda e: e.matmul(t[:, :], selr[:, g, :], qh[:, :], start=True, stop=False))
            pe.do(lambda e: e.matmul(t[:, :], selr[:, 4 + g, :], ql[:, :], start=False, stop=True), "qc")
            q = act if g % 2 else dve
            q.wait("qc", 4 * c + g + 1)
            if c >= 2:
                q.wait("S", 16 * (c - 1))
                for b in range(4 * c - 7, 4 * c - 3):
                    q.wait(f"qd{b % 3}", 64 * (b // 3 + 1))
            if g % 2:
                q.do(lambda e: e.copy(qc[c % 2][:, g, :], t[:, :]), s)
            else:
                q.do(lambda e: e.tensor_copy(qc[c % 2][:, g, :], t[:, :]), s)
            done[("qc", c, g)] = (s, sems.count[s])

        def KCOMB(c, g):
            pe.wait("c_sel", 4)
            pe.wait("kl", c + 1)
            t, s = misc.take(pe)
            pe.do(lambda e: e.matmul(t[:, 0:KC], selr[:, 8 + g, :], kh[:, :], start=True, stop=False))
            pe.do(lambda e: e.matmul(t[:, 0:KC], selr[:, 12 + g, :], kl[:, :], start=False, stop=True), "kc")
            act.wait("kc", 4 * c + g + 1)
            if c >= 2:
                act.wait("T", 16 * (c - 1))
                for b in range(4 * c - 7, 4 * c - 3):
                    act.wait(f"kd{b % 3}", 64 * (b // 3 + 1))
            act.do(lambda e: e.activation(kc[c % 2][:, g, :], t[:, 0:KC], ACT.Identity, bias=cols[:, 4:5]), s)
            done[("kc", c, g)] = (s, sems.count[s])

        def VP(c):
            pe.wait("ld_w", n_ldw)
            t, s = misc.take(pe)
            for i in range(4):
                pe.do(lambda e, i=i: e.matmul(t[0:CS, i * 128:(i + 1) * 128], cf[c % 2][:, i * CS:(i + 1) * CS], vwf[:, :],
                                              start=True, stop=True), "v" if i == 3 else None)
            dve.wait("v", c + 1)
            dve.wait("c_v9", 2)
            if c >= 2:
                dve.wait("Og", 16 * (c - 1))
            for i in range(4):
                dve.do(lambda e, i=i: e.tensor_tensor(v9[c % 2][:, i * H:(i + 1) * H, 0:8],
                                                      t[0:CS, i * 128:(i + 1) * 128].rearrange("p (h d) -> p h d", h=H),
                                                      vbb[:, :].rearrange("p (h d) -> p h d", h=H), ALU.add),
                       s if i == 3 else "v9")
            done[("v", c)] = (s, sems.count[s])

        def DIAG(b):
            c, i, s = b // 4, b % 4, b % 3
            for g in range(4):
                sp.wait(*done[("kc", c, g)])
            sp.wait("c_kd", 3)
            if b >= 3:
                sp.wait("S", 4 * (b - 2))
            for j in range(4):
                load(kd[s][32 * j:32 * j + 32, :, j, :].bitcast(F),
                     kc[c % 2][32 * j:32 * j + 32, :, i * CS:(i + 1) * CS].bitcast(F), f"kd{s}")
            for g in range(4):
                sp.wait(*done[("qc", c, g)])
            sp.wait("c_qd", 3)
            if b >= 3:
                sp.wait("T", 4 * (b - 2))
            for j in range(4):
                load(qd[s][32 * j:32 * j + 32, :, j, :].bitcast(F),
                     qc[c % 2][32 * j:32 * j + 32, :, i * S:(i + 1) * S].bitcast(F), f"qd{s}")

        def SC(b, g):
            c, i, s = b // 4, b % 4, b % 3
            pe.wait(*done[("qc", c, g)])
            pe.wait(f"kd{s}", 64 * (b // 3 + 1))
            t, f = bS.take(pe)
            pe.do(lambda e: e.matmul(t[:, 0:KC], qc[c % 2][:, g, i * S:(i + 1) * S], kd[s][:, g, :, :], start=True, stop=True), "S")
            dve.wait("S", 4 * b + g + 1)
            if b >= 2:
                dve.wait("mT", b - 1)
            dve.do(lambda e: e.tensor_reduce(mx[b % 2][:, 4 * g:4 * g + 4], t[:, 0:KC].rearrange("p (j m) -> p j m", j=4),
                                             AX.X, ALU.max, negate=True), f)
            done[("mx", b, g)] = (f, sems.count[f])

        def MT(b):
            for g in range(4):
                pe.wait(*done[("mx", b, g)])
            t, f = misc.take(pe)
            pe.do(lambda e: e.transpose(t[0:16, 0:128], mx[b % 2][:, :], idf[:, :]), "mT")
            act.wait("mT", b + 1)
            if b >= 2:
                act.wait(f"nm{b % 2}", 16 * (b // 2))
            act.do(lambda e: e.copy(nm[b % 2][:, :], t[0:16, 0:128]), f)
            sp.wait(f, sems.count[f])
            sp.wait(f"qd{b % 3}", 64 * (b // 3 + 1))
            load(qd[b % 3][24:25, :, :, :].rearrange("p g j n -> p (g j) n").bitcast(F), nm[b % 2][:, :].bitcast(F), f"nm{b % 2}")

        def ST(b, g):
            c, i, s, k = b // 4, b % 4, b % 3, 4 * b + g
            pe.wait(f"nm{b % 2}", 16 * (b // 2 + 1))
            t, f = bT.take(pe)
            pe.do(lambda e: e.matmul(t[0:CS, :], kc[c % 2][:, g, i * CS:(i + 1) * CS], qd[s][:, g, :, :], start=True, stop=True), "T")
            act.wait("T", k + 1)
            if k >= 3:
                act.wait("Og", k - 2)
            act.do(lambda e: e.activation(P[k % 3][:, :], t[0:CS, :], ACT.Exp), f)
            done[("p", b, g)] = (f, sems.count[f])

        def PV(b, g):
            c, i, k = b // 4, b % 4, 4 * b + g
            pe.wait(*done[("v", c)])
            pe.wait("c_o", 1)
            pe.wait(*done[("p", b, g)])
            if g == 0:
                PV.t, PV.f = bO.take(pe)
            t, f = PV.t, PV.f
            for j in range(4):
                pe.do(lambda e, j=j: e.matmul(t[32 * j:32 * j + 9, g * 128:(g + 1) * 128], v9[c % 2][:, i * H + 4 * g + j, :],
                                              P[k % 3][:, j * S:(j + 1) * S], start=True, stop=True),
                      "Og" if j == 3 else None)
            if g == 3:
                act.wait("Og", k + 1)
                if b >= 2:
                    act.wait("oX", b - 1)
                act.wait("c_z", 2)
                act.do(lambda e: e.copy(osb[b % 2][:, :, :], t[:, :]), f)
                done[("osb", b)] = (f, sems.count[f])

        def OT(b):
            pe.wait(*done[("osb", b)])
            t, f = bX.take(pe)
            for g in range(4):
                pe.do(lambda e, g=g: e.transpose(t[:, g * 128:(g + 1) * 128], osb[b % 2][:, g, :], idf[:, :]),
                      "oX" if g == 3 else None)
            v = t[:, :].rearrange("p (h r) -> p h r", r=32)
            dve.wait("oX", b + 1)
            if b >= 2:
                dve.wait(done[("on", b - 2)][0], done[("on", b - 2)][1])
            dve.do(lambda e: e.reciprocal(rd[b % 2][:, :], v[:, :, 8]), "rd")
            dve.wait("rd", b + 1)
            if b >= 2:
                dve.wait("onT", b - 1)
            dve.do(lambda e: e.tensor_tensor(on[b % 2][:, :].rearrange("p (h d) -> p h d", d=8), v[:, :, 0:8],
                                             rd[b % 2][:, :].unsqueeze(2).to_broadcast([128, 16, 8]), ALU.mult), f)
            done[("on", b)] = (f, sems.count[f])

        def ONT(b):
            pe.wait(*done[("on", b)])
            t, f = misc.take(pe)
            pe.do(lambda e: e.transpose(t[:, 0:128], on[b % 2][:, :], idf[:, :]), "onT")
            act.wait("onT", b + 1)
            if b >= 2:
                act.wait("pr", b - 1)
            act.do(lambda e: e.copy(oT[b % 2][:, :], t[:, 0:128]), f)
            done[("oT", b)] = (f, sems.count[f])

        def PR(b):
            c, i = b // 4, b % 4
            pe.wait(*done[("oT", b)])
            t, f = misc.take(pe)
            pe.do(lambda e: e.matmul(t[:, 0:128], oT[b % 2][:, :], pwf[:, :], start=True, stop=True), "pr")
            dve.wait("pr", b + 1)
            dve.wait("xp", 4 * c + 4)
            if c >= 3:
                dve.wait("xr", 4 * (c - 2))
            dve.do(lambda e: e.tensor_tensor(x1[c % 3][:, i, :], t[:, 0:128], xin[c % 4][:, i, :], ALU.add), f)
            done[("x1", b)] = (f, sems.count[f])

        def N2a(c):
            for b in range(4 * c, 4 * c + 4):
                dve.wait(*done[("x1", b)])
            norm_stats(c, 1, x1[c % 3])

        def N2b(c):
            if c >= 2:
                dve.wait("xr", 4 * (c - 1))
            norm_apply(c, 1, hh[c % 2], x1[c % 3], "hh")
            pool.wait("hh", 4 * c + 4)
            if c >= 2:
                pool.wait(f"sx{c % 2}", 16 * (c // 2))
            for i in range(4):
                pool.do(lambda e, i=i: e.tensor_tensor(xr[c % 2][:, i, :], x1[c % 3][:, i, :], hh[c % 2][:, i, :], ALU.add), "xr")
            sp.wait("xr", 4 * c + 4)
            load(xres[c], xr[c % 2][:, :, :].rearrange("p a b -> p (a b)"), f"sx{c % 2}")

        def N3a(c):
            dve.wait("hh", 4 * c + 4)
            norm_stats(c, 2, hh[c % 2])

        def N3b(c):
            if c >= 2:
                dve.wait("zT", c - 1)
            norm_apply(c, 2, zz[c % 2], hh[c % 2], "zz")

        def ZT(c):
            pe.wait("zz", 4 * c + 4)
            t, f = misc.take(pe)
            for i in range(4):
                pe.do(lambda e, i=i: e.transpose(t[:, i * 128:(i + 1) * 128], zz[c % 2][:, i, :], idf[:, :]),
                      "zT" if i == 3 else None)
            act.wait("zT", c + 1)
            act.do(lambda e: e.activation(xnT[:, c * TC:(c + 1) * TC], t[:, :], ACT.Identity, bias=cols[:, 3:4],
                                          scale=cols[:, 2:3]), f)
            dve.wait(f, sems.count[f])
            dve.wait("rt", c)
            dve.do(lambda e: e.tensor_copy(zh[:, :], xnT[:, c * TC:(c + 1) * TC]), "zh")
            dve.wait("zh", c + 1)
            dve.do(lambda e: e.tensor_tensor(zl[:, :], xnT[:, c * TC:(c + 1) * TC], zh[:, :].bitcast(F), ALU.subtract), "zl")

        def RT(c):
            pe.wait("zl", c + 1)
            t, f = misc.take(pe)
            three(pe, t[:, :], (rwh[:, :], rwl[:, :]), (zh[:, :], zl[:, :]), "rt")
            act.wait("rt", c + 1)
            act.wait("lT", c)
            act.do(lambda e: e.copy(lg[:, :], t[0:8, :]), f)
            done[("lg", c)] = (f, sems.count[f])

        def LT(c):
            b = c % 2
            pe.wait(*done[("lg", c)])
            t, f = misc.take(pe)
            for i in range(4):
                pe.do(lambda e, i=i: e.transpose(t[:, i * 8:(i + 1) * 8], lg[:, i * 128:(i + 1) * 128], idf[0:8, 0:8]),
                      "lT" if i == 3 else None)
            v = t[:, 0:32].rearrange("p (i e) -> p i e", e=8)
            dve.wait("lT", c + 1)
            dve.do(lambda e: e.tensor_reduce(s4[b][:, 0, :], v, AX.X, ALU.max), "r1")
            dve.wait("r1", c + 1)
            dve.do(lambda e: e.tensor_tensor(sm[b][:, 0, :, :], v, s4[b][:, 0, :].unsqueeze(2).to_broadcast([128, 4, 8]),
                                             ALU.subtract), f)
            act.wait(f, sems.count[f])
            act.do(lambda e: e.activation(sm[b][:, 1, :, :], sm[b][:, 0, :, :], ACT.Exp, scale=1.0 / TEMP), "r2")

        def TOP(c):
            b = c % 2
            dve.wait("r2", c + 1)
            dve.do(lambda e: e.tensor_reduce(s4[b][:, 1, :], sm[b][:, 1, :, :], AX.X, ALU.add), "r3")
            dve.wait("r3", c + 1)
            dve.do(lambda e: e.reciprocal(s4[b][:, 2, :], s4[b][:, 1, :]), "r4")
            dve.wait("r4", c + 1)
            dve.do(lambda e: e.tensor_tensor(sm[b][:, 2, :, :], sm[b][:, 1, :, :],
                                             s4[b][:, 2, :].unsqueeze(2).to_broadcast([128, 4, 8]), ALU.mult), "r5")
            dve.wait("r5", c + 1)
            for i in range(4):
                dve.do(lambda e, i=i: e.max(m8[b][:, i, :], sm[b][:, 2, i, :]), "r6")
            dve.wait("r6", 4 * c + 4)
            for i in range(4):
                dve.do(lambda e, i=i: e.max_index(i8[b][:, i, :], m8[b][:, i, :], sm[b][:, 2, i, :]), "r7")
            dve.wait("r7", 4 * c + 4)
            dve.do(lambda e: e.tensor_copy(if8[b][:, :, :], i8[b][:, :, :]), "r8")
            dve.wait("r8", c + 1)
            for k in range(2):
                dve.do(lambda e, k=k: e.tensor_tensor(sm[b][:, 3 * k, :, :], iot[:, :, :],
                                                      if8[b][:, :, k].unsqueeze(2).to_broadcast([128, 4, 8]),
                                                      ALU.is_equal), "r9")
            dve.wait("r9", 2 * c + 2)
            dve.do(lambda e: e.tensor_tensor(sm[b][:, 0, :, :], sm[b][:, 0, :, :], sm[b][:, 3, :, :], ALU.add), "r10")
            dve.wait("r10", c + 1)
            if c >= 2:
                dve.wait("wT", c - 1)
            dve.do(lambda e: e.tensor_tensor(wd[b][:, :, :], sm[b][:, 0, :, :], sm[b][:, 2, :, :], ALU.mult), "wd")

        def WT(c):
            b = c % 2
            pe.wait("wd", c + 1)
            t, f = misc.take(pe)
            pe.do(lambda e: e.transpose(t[0:32, 0:128], wd[b][:, :, :].rearrange("p a b -> p (a b)"), idf[:, :]), "wT")
            act.wait("wT", c + 1)
            if c >= 2:
                act.wait(f"sw{b}", 16 * (c // 2))
            act.do(lambda e: e.copy(wts[b][:, :], t[0:32, 0:128]), f)
            sp.wait(f, sems.count[f])
            load(wsc[c], wts[b][:, :], f"sw{b}")

        for t in range(-8, NB + 16):
            c0, i = divmod(t, 4)

            def front(fn, lead, at, *a):
                c = c0 + lead
                if i == at and 0 <= c < NC:
                    return fn(c, *a)

            front(LX, 2, 2)
            ok = lambda b: 0 <= b < NB
            if ok(t + 1):
                DIAG(t + 1)
            if ok(t):
                SC(t, 0)
                SC(t, 1)
            if ok(t - 1):
                ST(t - 1, 0)
            if ok(t):
                SC(t, 2)
            if ok(t - 1):
                ST(t - 1, 1)
            if ok(t):
                SC(t, 3)
            if ok(t - 1):
                PV(t - 1, 0)
                ST(t - 1, 2)
            if ok(t - 2):
                OT(t - 2)
            if ok(t - 1):
                PV(t - 1, 1)
            if i == 0 and 0 <= c0 + 1 < NC:
                XT(c0 + 1)
            front(QP, 1, 1)
            if i == 2 and 0 <= c0 + 1 < NC:
                QC(c0 + 1, 0)
                KCOMB(c0 + 1, 0)
            if ok(t):
                MT(t)
            if ok(t - 1):
                ST(t - 1, 3)
                PV(t - 1, 2)
            front(CT, 1, 0)
            front(KP, 1, 1)
            if i == 2 and 0 <= c0 + 1 < NC:
                QC(c0 + 1, 1)
                KCOMB(c0 + 1, 1)
                QC(c0 + 1, 2)
            if ok(t - 2):
                ONT(t - 2)
            if ok(t - 1):
                PV(t - 1, 3)
            if i == 2 and 0 <= c0 + 1 < NC:
                KCOMB(c0 + 1, 2)
                QC(c0 + 1, 3)
                KCOMB(c0 + 1, 3)
                VP(c0 + 1)
            if ok(t - 2):
                PR(t - 2)
            front(LN1, 2, 2)
            front(XH, 2, 3)
            front(N2a, -2, 1)
            front(N2b, -2, 2)
            front(N3a, -2, 2)
            front(N3b, -2, 3)
            front(ZT, -3, 0)
            front(RT, -3, 1)
            front(LT, -3, 2)
            front(TOP, -3, 2)
            front(WT, -3, 3)

        endA = {k: v for k, v in sems.count.items() if v}
        sa.close()
        pa.close()

        sb_, pb_ = ExitStack(), ExitStack()
        nb = [0]

        def Bt(shape, dt=F, n=1):
            nb[0] += 1
            ts = [sbt(sb_, f"b{nb[0]}_{i}", shape, dt) for i in range(n)]
            return ts[0] if n == 1 else ts

        w1h, w1l, w2h, w2l = (Bt([128, E, 512], R) for _ in range(4))
        wraw = Bt([128, 2, 512], F, 2)
        gh, gl = Bt([128, TC], R, 2), Bt([128, TC], R, 2)
        sf, sh, sl = Bt([128, TC], F, 3), Bt([128, TC], R, 6), Bt([128, TC], R, 6)
        wb = Bt([128, TC], F, 4)
        ty = Bt([128, TC], F, 2)
        acc = Bt([128, TC], F, 2)
        xo = Bt([128, TC], F, 2)
        oo = Bt([128, TC], F, 2)
        bH, bY, bF = Banks("bH", pt(pb_, "qh", 4)), InOrder("yw", pt(pb_, "qy", 2)), InOrder("oo", pt(pb_, "qf", 1))

        for q in (pe, act, dve, sp):
            for k, v in endA.items():
                q.wait(k, v)

        W2v = W2.rearrange("e (k p) d -> e p k d", p=128)

        def WL(e_):
            s = e_ % 2
            if e_ >= 2:
                sp.wait("wlo", 2 * (e_ - 1))
            load(wraw[s][:, 0, :], W1[e_], f"wr{s}")
            load(wraw[s][:, 1, :].rearrange("p (k d) -> p k d", k=4), W2v[e_], f"wr{s}")

        def WS(e_):
            s = e_ % 2
            dve.wait(f"wr{s}", 32 * (e_ // 2 + 1))
            for hi, k in ((w1h, 0), (w2h, 1)):
                dve.do(lambda e, hi=hi, k=k: e.tensor_copy(hi[:, e_, :], wraw[s][:, k, :]), "whi")
            dve.wait("whi", 2 * e_ + 2)
            for hi, lo, k in ((w1h, w1l, 0), (w2h, w2l, 1)):
                dve.do(lambda e, hi=hi, lo=lo, k=k: e.tensor_tensor(lo[:, e_, :], wraw[s][:, k, :], hi[:, e_, :].bitcast(F),
                                                                  ALU.subtract), "wlo")

        def GP(c):
            s = c % 2
            if c >= 2:
                dve.wait("M1", 32 * (c - 1))
            dve.do(lambda e: e.tensor_copy(gh[s][:, :], xnT[:, c * TC:(c + 1) * TC]), "gh")
            dve.wait("gh", c + 1)
            dve.do(lambda e: e.tensor_tensor(gl[s][:, :], xnT[:, c * TC:(c + 1) * TC], gh[s][:, :].bitcast(F), ALU.subtract), "gl")

        def WB(u):
            c, e_, s = u // E, u % E, u % 4
            if u >= 4:
                sp.wait("yw", u - 3)
            src = wsc[c].rearrange("(t e) n -> e t n", t=4)[e_].partition_broadcast(128)
            load(wb[s][:, :].rearrange("p (t n) -> p t n", t=4), src, f"wb{s}")

        def M1(u, f):
            c, e_, k = u // E, u % E, 4 * u + f
            pe.wait("wlo", 2 * min(u + 1, E))
            pe.wait("gl", c + 1)
            t, s = bH.take(pe)
            fs = slice(f * 128, (f + 1) * 128)
            three(pe, t[:, :], (w1h[:, e_, fs], w1l[:, e_, fs]), (gh[c % 2][:, :], gl[c % 2][:, :]), "M1")
            act.wait("M1", k + 1)
            if k >= 3:
                act.wait("sl", k - 2)
            act.do(lambda e: e.activation(sf[k % 3][:, :], t[:, :], ACT.Silu), "sf")
            if k >= 6:
                act.wait("M2", k - 5)
            act.do(lambda e: e.activation(sh[k % 6][:, :], t[:, :], ACT.Silu), s)
            dve.wait("sf", k + 1)
            dve.wait(s, sems.count[s])
            if k >= 6:
                dve.wait("M2", k - 5)
            dve.do(lambda e: e.tensor_tensor(sl[k % 6][:, :], sf[k % 3][:, :], sh[k % 6][:, :].bitcast(F), ALU.subtract), "sl")

        def M2(u, f):
            c, e_, k = u // E, u % E, 4 * u + f
            pe.wait("sl", k + 1)
            if f == 0:
                M2.t, _ = bY.take(pe)
            t = M2.t
            fs = slice(f * 128, (f + 1) * 128)
            pe.do(lambda e: e.matmul(t[:, :], w2l[:, e_, fs], sh[k % 6][:, :], start=(f == 0), stop=False))
            pe.do(lambda e: e.matmul(t[:, :], w2h[:, e_, fs], sh[k % 6][:, :], start=False, stop=False))
            pe.do(lambda e: e.matmul(t[:, :], w2h[:, e_, fs], sl[k % 6][:, :], start=False, stop=(f == 3)), "M2")

        def YW(u):
            c, e_, s = u // E, u % E, u % 4
            t = M2.t
            dve.wait("M2", 4 * u + 4)
            dve.wait(f"wb{s}", 16 * (u // 4 + 1))
            if e_ == 0:
                if c >= 2:
                    dve.wait("fT", c - 1)
                dve.do(lambda e: e.tensor_tensor(acc[c % 2][:, :], t[:, :], wb[s][:, :], ALU.mult), "yw")
            else:
                dve.do(lambda e: e.tensor_tensor(ty[u % 2][:, :], t[:, :], wb[s][:, :], ALU.mult), "yw")
            dve.wait("yw", u + 1)
            if e_:
                if e_ > 1:
                    dve.wait("ac", c * 7 + e_ - 1)
                dve.do(lambda e: e.tensor_tensor(acc[c % 2][:, :], acc[c % 2][:, :], ty[u % 2][:, :], ALU.add), "ac")

        def XO(c):
            s = c % 2
            if c >= 2:
                sp.wait("oo", c - 1)
            load(xo[s][:, :], xres[c], f"xo{s}")

        def FIN(c):
            s = c % 2
            pe.wait("ac", 7 * c + 7)
            t, f = bF.take(pe)
            for i in range(4):
                pe.do(lambda e, i=i: e.transpose(t[:, i * 128:(i + 1) * 128], acc[s][:, i * 128:(i + 1) * 128], idf[:, :]),
                      "fT" if i == 3 else None)
            dve.wait("fT", c + 1)
            dve.wait(f"xo{s}", 16 * (c // 2 + 1))
            if c >= 2:
                dve.wait(f"so{s}", 16 * (c // 2))
            dve.do(lambda e: e.tensor_tensor(oo[s][:, :], t[:, :], xo[s][:, :], ALU.add), "oo")
            sp.wait("oo", c + 1)
            load(out[4 * c:4 * c + 4].rearrange("b n d -> n b d"), oo[s][:, :].rearrange("p (b d) -> p b d", b=4), f"so{s}")

        WL(0)
        WL(1)
        WB(0)
        WB(1)
        GP(0)
        NU = NC * E
        LAG = 3
        for k in range(4 * NU + LAG + 1):
            u, f = divmod(k, 4)
            c, e_ = divmod(u, E)
            if u < NU:
                if f == 0:
                    if u < E:
                        WS(u)
                        if u + 2 < E:
                            WL(u + 2)
                    if u + 2 < NU:
                        WB(u + 2)
                    if e_ == 4:
                        XO(c)
                        if c + 1 < NC:
                            GP(c + 1)
                M1(u, f)
            k2 = k - LAG
            if 0 <= k2 < 4 * NU:
                u2, f2 = divmod(k2, 4)
                M2(u2, f2)
                if f2 == 3:
                    YW(u2)
            if k >= 4 * E and (k - 4 * E) % (4 * E) == 6:
                FIN((k - 4 * E) // (4 * E))
        FIN(NC - 1)
        for s in range(2):
            sp.wait(f"so{s}", 16 * (NC // 2))
            sp.wait(f"sx{s}", 16 * (NC // 2))
            sp.wait(f"sw{s}", 16 * (NC // 2))

        block = st.enter_context(nc.Block())

        @block.sync
        def _(e):
            sp.emit(e)

        @block.tensor
        def _(e):
            pe.emit(e)

        @block.scalar
        def _(e):
            act.emit(e)

        @block.vector
        def _(e):
            dve.emit(e)

        @block.gpsimd
        def _(e):
            pool.emit(e)

        pb_.close()
        sb_.close()


def _selectors():
    import numpy as np
    sel = np.zeros((128, 16, 128), np.float32)
    for kind, parts in enumerate(((0, 2), (1,), (0, 1), (2,))):
        for g in range(4):
            for j in range(4):
                for d in range(HD):
                    for p in parts:
                        sel[(4 * g + j) * HD + d, 4 * kind + g, 32 * j + 8 * p + d] = 1.0
    return sel


def kernel(**inputs):
    import numpy as np
    import concourse.bacc as bacc
    from concourse.bass_utils import run_bass_kernel_spmd

    i = {k: np.asarray(v) for k, v in inputs.items()}
    col = lambda a: a.reshape(128, 1)
    rows = lambda a, n: np.broadcast_to(a.reshape(1, 128), (n, 128))
    one24 = np.zeros((128, 1), np.float32)
    one24[24] = 1.0
    iota = np.broadcast_to(np.arange(8, dtype=np.float32), (128, 4, 8))
    args = [
        ("x", i["x"]), ("ctx", i["ctx_768"]), ("qw", i["L0_xattn_q_w"]), ("qb", col(i["L0_xattn_q_b"])),
        ("kw", i["L0_xattn_kv_w"][:, 0:128]), ("kb", col(i["L0_xattn_kv_b"][0:128])),
        ("vw", i["L0_xattn_kv_w"][:, 128:256]), ("vb", rows(i["L0_xattn_kv_b"][128:256], CS)),
        ("pw", i["L0_xattn_proj_w"]), ("pb", rows(i["L0_xattn_proj_b"], 128)),
        ("gam", col(i["L0_ffn_gamma"])), ("bet", col(i["L0_ffn_beta"])), ("rwT", i["L0_ffn_router_w"].T),
        ("W1", i["L0_ffn_W1"]), ("W2", i["L0_ffn_W2"]), ("ident", np.eye(128, dtype=np.float32)),
        ("sel", _selectors()), ("one24", one24), ("iota", iota),
    ]
    nc = bacc.Bacc("TRN2", target_bir_lowering=False, num_devices=1)
    arrays, aps = {}, []
    for name, a in args:
        a = np.ascontiguousarray(a)
        arrays[f"in_{name}"] = a
        aps.append(nc.dram_tensor(f"in_{name}", a.shape, mybir.dt.from_np(a.dtype), kind="ExternalInput").ap())
    o = nc.dram_tensor("out_0", (NB, S, D), F, kind="ExternalOutput").ap()
    xattn_moe(nc, *aps, o)
    r = run_bass_kernel_spmd(nc, [arrays], core_ids=[0])
    return r.results[0]["out_0"]
```

```python
from contextlib import ExitStack

import concourse.bass as bass
from concourse import mybir

F = mybir.dt.float32
R = mybir.dt.float32r
U32 = mybir.dt.uint32
ALU = mybir.AluOpType
ACT = mybir.ActivationFunctionType
AX = mybir.AxisListType

NB, S, D = 64, 128, 128
CS, CD = 77, 96
H, HD = 16, 8
E, FF = 8, 512
NC = NB // 4
TC = 4 * S
KC = 4 * CS
SCALE = float(HD) ** -0.5
EPS = 1e-5
TEMP = 1.5


class Queue:

    def __init__(self, sems):
        self.items, self.sems, self.seen = [], sems, {}

    def wait(self, name, value):
        if value > self.seen.get(name, 0):
            self.seen[name] = value
            self.items.append((name, value))

    def do(self, fn, sem=None, n=1):
        self.items.append((fn, sem, n))
        if sem is not None:
            self.sems.count[sem] = self.sems.count.get(sem, 0) + n

    def emit(self, eng):
        for it in self.items:
            if isinstance(it[0], str):
                eng.wait_ge(self.sems[it[0]], it[1])
            else:
                ins = it[0](eng)
                if it[1] is not None:
                    ins.then_inc(self.sems[it[1]], it[2])


class Sems:

    def __init__(self, nc, ctx):
        self.nc, self.ctx, self.count, self.made = nc, ctx, {}, {}

    def __getitem__(self, name):
        if name not in self.made:
            self.made[name] = self.ctx.enter_context(self.nc.semaphore("s_" + name))
        return self.made[name]


class Banks:

    def __init__(self, name, tiles):
        self.name, self.tiles, self.n = name, tiles, 0

    def take(self, q):
        k = self.n
        self.n += 1
        slot, use = k % len(self.tiles), k // len(self.tiles)
        q.wait(f"{self.name}{slot}", use)
        return self.tiles[slot], f"{self.name}{slot}"


class InOrder(Banks):

    def take(self, q):
        k = self.n
        self.n += 1
        q.wait(self.name, k - len(self.tiles) + 1)
        return self.tiles[k % len(self.tiles)], self.name


def xattn_moe(nc, x, ctx_in, qw, qb, kw, kb, vw, vb, pw, pb, gam, bet, rwT, W1, W2, ident, sel, one24, iota, out):
    st = ExitStack()
    with st:
        sems = Sems(nc, st)
        pe, act, dve, pool, sp = (Queue(sems) for _ in range(5))

        def sbt(ctx, name, shape, dt=F):
            return ctx.enter_context(nc.sbuf_tensor(name, shape, dt))

        xres = nc.dram_tensor("xres", (NC, 128, 512), F, kind="Internal").ap()
        wsc = nc.dram_tensor("wsc", (NC, 32, 128), F, kind="Internal").ap()

        xnT = sbt(st, "xnT", [128, NC * TC])
        idf = sbt(st, "idf", [128, 128])

        sa = ExitStack()
        nm_ = [0]

        def A(shape, dt=F, n=1):
            nm_[0] += 1
            ts = [sbt(sa, f"a{nm_[0]}_{i}", shape, dt) for i in range(n)]
            return ts[0] if n == 1 else ts

        selr = A([128, 16, 128], R)
        qwh, qwl, rwh, rwl = (A([128, 128], R) for _ in range(4))
        kwh, kwl = (A([CD, 128], R) for _ in range(2))
        vwf = A([CD, 128])
        pwf = A([128, 128])
        vbb = A([CS, 128])
        pbb = A([128, 128])
        cols = A([128, 8])
        iot = A([128, 4, 8])
        nhalf = A([128, 4])
        xin = A([128, 4, 128], F, 4)
        cin = A([CS, 4, CD], F, 3)
        xh = A([128, 4, 128], F, 2)
        xTh = A([128, TC], R)
        xTl = A([128, TC], R)
        cf = A([CD, KC], F, 2)
        ch, cl = A([CD, KC], R), A([CD, KC], R)
        qf = A([128, TC])
        qh, ql = A([128, TC], R), A([128, TC], R)
        kf = A([128, KC])
        kh, kl = A([128, KC], R), A([128, KC], R)
        qc = A([128, 4, 4, S], R, 2)
        kc = A([128, 4, 4, CS], R, 2)
        qd = A([128, 2, 4, 4, S], R, 2)
        kd = A([128, 2, 4, 4, CS], R, 2)
        v9 = A([CS, 4 * H, 9], F, 2)
        P = A([CS, 4 * S], F, 4)
        mx = A([128, 16], F, 2)
        nm = A([16, 128], R, 2)
        osb = A([128, 4, 128], F, 2)
        rd = A([128, 16], F, 2)
        on = A([128, 128], F, 2)
        oT = A([128, 128], F, 2)
        x1 = A([128, 4, 128], F, 3)
        hh = A([128, 4, 128], F, 2)
        zz = A([128, 4, 128], F, 2)
        xr = A([128, 4, 128], F, 2)
        stg, wst = zz, hh[0]
        bst = A([128, 3, 4, 6])
        mv = A([128, 3, 4, 2], F, 2)
        rs = A([128, 3, 4], F, 2)
        ve = A([128, 3, 4], F, 2)
        ng = A([128, 3, 4], F, 2)
        zh, zl = A([128, TC], R), A([128, TC], R)
        lg = A([8, TC])
        sm = A([128, 4, 4, 8], F, 2)
        s4 = A([128, 3, 4], F, 2)
        m8 = A([128, 4, 8], F, 2)
        i8 = A([128, 4, 8], U32, 2)
        if8 = A([128, 4, 8], F, 2)
        wd = A([128, 4, 8], F, 2)
        wts = A([32, 128], F, 2)

        pa = ExitStack()

        def pt(ctx, name, n):
            return [ctx.enter_context(nc.psum_tensor(f"{name}{i}", [128, 512], F)) for i in range(n)]

        misc, bS, bT = Banks("misc", pt(pa, "pm", 3)), Banks("bS", pt(pa, "ps", 2)), Banks("bT", pt(pa, "pt", 2))
        bO = Banks("bO", pt(pa, "po", 1))

        def load(dst, src, sem):
            sp.do(lambda e: e.dma_start(dst, src), sem, 16)

        load(idf[:, :], ident, "ld_id")
        for t, (dst, src) in enumerate(((wst[:, 0, :], qw), (wst[0:CD, 1, :], kw), (wst[:, 2, 0:8], rwT), (vwf[:, :], vw),
                                        (pwf[:, :], pw), (vbb[:, :], vb), (pbb[:, :], pb), (cols[:, 0:1], qb),
                                        (cols[:, 1:2], kb), (cols[:, 2:3], gam), (cols[:, 3:4], bet),
                                        (cols[:, 4:5], one24), (iot[:, :, :], iota))):
            load(dst, src, "ld_w")
        n_ldw = sems.count["ld_w"]

        dve.do(lambda e: e.memset(bO.tiles[0][:, :], 0.0), "c_o")
        dve.do(lambda e: e.memset(nhalf[:, :], -0.5), "c_nh")
        for i in range(2):
            dve.do(lambda e, i=i: e.memset(v9[i][:, :, :], 1.0), "c_v9")
            dve.do(lambda e, i=i: e.memset(osb[i][:, :, :], 0.0), "c_z")
        for i in range(2):
            pool.do(lambda e, i=i: e.memset(kd[i][:, :, :, :, :].bitcast(F), 0.0), "c_kd")
        for i in range(2):
            pool.do(lambda e, i=i: e.memset(qd[i][:, :, :, :, :].bitcast(F), 0.0), "c_qd")
        dve.do(lambda e: e.memset(rwh[:, :].bitcast(F), 0.0), "c_rw")
        dve.do(lambda e: e.memset(rwl[:, :].bitcast(F), 0.0), "c_rw")
        dve.wait("ld_w", n_ldw)
        dve.wait("c_rw", 2)
        dve.do(lambda e: e.tensor_scalar(cols[:, 0:1], cols[:, 0:1], SCALE, None, ALU.mult), "c_qb")
        for hi, src, k in ((qwh[:, :], wst[:, 0, :], "qw"), (kwh[:, :], wst[0:CD, 1, :], "kw"), (rwh[:, 0:8], wst[:, 2, 0:8], "rw")):
            dve.do(lambda e, hi=hi, src=src: e.tensor_copy(hi, src), "c_hi")
        dve.wait("c_hi", 3)
        for hi, lo, src in ((qwh[:, :], qwl[:, :], wst[:, 0, :]), (kwh[:, :], kwl[:, :], wst[0:CD, 1, :]),
                            (rwh[:, 0:8], rwl[:, 0:8], wst[:, 2, 0:8])):
            dve.do(lambda e, hi=hi, lo=lo, src=src: e.tensor_tensor(lo, src, hi.bitcast(F), ALU.subtract), "c_lo")
        for g in range(4):
            if g >= 2:
                sp.wait("c_sel", g - 1)
            load(stg[g % 2][:, :, :], sel[:, 4 * g:4 * g + 4, :], f"ld_sel{g % 2}")
            act.wait(f"ld_sel{g % 2}", 16 * (g // 2 + 1))
            act.do(lambda e, g=g: e.copy(selr[:, 4 * g:4 * g + 4, :], stg[g % 2][:, :, :]), "c_sel")

        done = {}

        def LX(c):
            if c >= 4:
                sp.wait(*done[("x1", 4 * (c - 4) + 3)])
            load(xin[c % 4][:, :, :], x[4 * c:4 * c + 4].rearrange("b n d -> n b d"), f"lx{c % 4}")
            if c >= 3:
                sp.wait("cT", c - 2)
            load(cin[c % 3][:, :, :], ctx_in[4 * c:4 * c + 4].rearrange("b m d -> m b d"), f"lc{c % 3}")

        def norm_stats(c, k, src):
            b = c % 2

            def stats(*i4):
                if c >= 1:
                    dve.wait(f"mv{k}", 4 * c)
                for i in i4:
                    dve.do(lambda e, i=i: e.bn_stats(bst[:, k, i, :], src[:, i, :]), f"bst{k}")

            def aggr():
                dve.wait(f"bst{k}", 4 * c + 4)
                if c >= 2:
                    dve.wait(f"rs{k}", c - 1)
                    dve.wait(f"nm_{k}", c - 1)
                for i in range(4):
                    dve.do(lambda e, i=i: e.bn_aggr(mv[b][:, k, i, :], bst[:, k, i, :]), f"mv{k}")
                pool.wait("c_nh", 1)
                pool.wait(f"mv{k}", 4 * c + 4)
                pool.do(lambda e: e.tensor_scalar(ve[b][:, k, :], mv[b][:, k, :, 1], EPS, None, ALU.add), f"ve{k}")
                pool.do(lambda e: e.tensor_scalar(ng[b][:, k, :], mv[b][:, k, :, 0], -1.0, None, ALU.mult), f"nm_{k}")
                pool.wait(f"ve{k}", c + 1)
                pool.do(lambda e: e.tensor_tensor(rs[b][:, k, :], ve[b][:, k, :], nhalf[:, :], ALU.pow), f"rs{k}")

            return [lambda: stats(0, 1), lambda: stats(2, 3), aggr]

        def norm_apply(c, k, dst, src, sem):
            b = c % 2
            pool.wait(f"rs{k}", c + 1)
            for i in range(4):
                pool.do(lambda e, i=i: e.tensor_scalar(dst[:, i, :], src[:, i, :], ng[b][:, k, i:i + 1], rs[b][:, k, i:i + 1],
                                                       ALU.add, ALU.mult), sem)

        def XH(c):
            if c >= 2:
                pool.wait("xT", c - 1)
            pool.wait(f"lx{c % 4}", 16 * (c // 4 + 1))
            norm_apply(c, 0, xh[c % 2], xin[c % 4], "xh")

        def XP(c):
            pool.wait("ld_w", n_ldw)
            pool.wait("xh", 4 * c + 4)
            for i in range(4):
                pool.do(lambda e, i=i: e.tensor_tensor(xin[c % 4][:, i, :], xin[c % 4][:, i, :], pbb[:, :], ALU.add), "xp")

        def LN1(c):
            steps = norm_stats(c, 0, xin[c % 4])
            return [lambda: dve.wait(f"lx{c % 4}", 16 * (c // 4 + 1)) or steps[0]()] + steps[1:]

        def XH(c):
            if c >= 2:
                dve.wait("xT", c - 1)
            norm_apply(c, 0, xh[c % 2], xin[c % 4], "xh")

        def XP(c):
            pool.wait("ld_w", n_ldw)
            pool.wait("xh", 4 * c + 4)
            for i in range(4):
                pool.do(lambda e, i=i: e.tensor_tensor(xin[c % 4][:, i, :], xin[c % 4][:, i, :], pbb[:, :], ALU.add), "xp")

        def XT(c):
            pe.wait("ld_id", 16)
            pe.wait("xh", 4 * c + 4)
            t, s = misc.take(pe)
            for i in range(4):
                pe.do(lambda e, i=i: e.transpose(t[:, i * 128:(i + 1) * 128], xh[c % 2][:, i, :], idf[:, :]),
                      "xT" if i == 3 else None)
            act.wait("xT", c + 1)
            act.wait("q", c)
            act.do(lambda e: e.copy(xTh[:, :], t[:, :]), "xTh")
            dve.wait("xTh", c + 1)
            dve.do(lambda e: e.tensor_tensor(xTl[:, :], t[:, :], xTh[:, :].bitcast(F), ALU.subtract), s)
            done[("xTl", c)] = (s, sems.count[s])

        def three(pe, out, w, xs, sem):
            (wh, wl), (xh_, xl) = w, xs
            pe.do(lambda e: e.matmul(out, wl, xh_, start=True, stop=False))
            pe.do(lambda e: e.matmul(out, wh, xh_, start=False, stop=False))
            pe.do(lambda e: e.matmul(out, wh, xl, start=False, stop=True), sem)


        def QP(c):
            pe.wait("c_lo", 3)
            pe.wait(*done[("xTl", c)])
            t, s = misc.take(pe)
            three(pe, t[:, :], (qwh[:, :], qwl[:, :]), (xTh[:, :], xTl[:, :]), "q")
            act.wait("c_qb", 1)
            act.wait("q", c + 1)
            act.wait("ql", c)
            act.do(lambda e: e.activation(qf[:, :], t[:, :], ACT.Identity, bias=cols[:, 0:1], scale=SCALE), s)
            done[("qf", c)] = (s, sems.count[s])

        def QH(c):
            dve.wait(*done[("qf", c)])
            dve.wait("qc", 4 * c)
            dve.do(lambda e: e.tensor_copy(qh[:, :], qf[:, :]), "qh")

        def QL(c):
            dve.wait("qh", c + 1)
            dve.do(lambda e: e.tensor_tensor(ql[:, :], qf[:, :], qh[:, :].bitcast(F), ALU.subtract), "ql")

        def CT(c):
            pe.wait(f"lc{c % 3}", 16 * (c // 3 + 1))
            t, s = misc.take(pe)
            for i in range(4):
                pe.do(lambda e, i=i: e.transpose(t[0:CD, i * CS:(i + 1) * CS], cin[c % 3][:, i, :], idf[0:CS, 0:CS]),
                      "cT" if i == 3 else None)
            act.wait("cT", c + 1)
            if c >= 2:
                act.wait("v", c - 1)
            act.do(lambda e: e.copy(cf[c % 2][:, :], t[0:CD, 0:KC]), s)
            done[("cf", c)] = (s, sems.count[s])

        def CH(c):
            dve.wait(*done[("cf", c)])
            dve.wait("k", c)
            dve.do(lambda e: e.tensor_copy(ch[:, :], cf[c % 2][:, :]), "ch")

        def CL(c):
            dve.wait("ch", c + 1)
            dve.do(lambda e: e.tensor_tensor(cl[:, :], cf[c % 2][:, :], ch[:, :].bitcast(F), ALU.subtract), "cl")

        def KP(c):
            pe.wait("cl", c + 1)
            t, s = misc.take(pe)
            three(pe, t[:, 0:KC], (kwh[:, :], kwl[:, :]), (ch[:, :], cl[:, :]), "k")
            act.wait("k", c + 1)
            act.wait("kl", c)
            act.do(lambda e: e.activation(kf[:, :], t[:, 0:KC], ACT.Identity, bias=cols[:, 1:2]), s)
            done[("kf", c)] = (s, sems.count[s])

        def KH(c):
            dve.wait(*done[("kf", c)])
            dve.wait("kc", 4 * c)
            dve.do(lambda e: e.tensor_copy(kh[:, :], kf[:, :]), "kh")

        def KL(c):
            dve.wait("kh", c + 1)
            dve.do(lambda e: e.tensor_tensor(kl[:, :], kf[:, :], kh[:, :].bitcast(F), ALU.subtract), "kl")

        def QC(c, g):
            pe.wait("c_sel", 4)
            pe.wait("ql", c + 1)
            t, s = misc.take(pe)
            pe.do(lambda e: e.matmul(t[:, :], selr[:, g, :], qh[:, :], start=True, stop=False))
            pe.do(lambda e: e.matmul(t[:, :], selr[:, 4 + g, :], ql[:, :], start=False, stop=True), "qc")
            q = act if g % 2 else dve
            q.wait("qc", 4 * c + g + 1)
            if c >= 2:
                q.wait("S", 16 * (c - 1))
                for p in (2 * c - 4, 2 * c - 3):
                    q.wait(f"qd{p % 2}", 64 * (p // 2 + 1))
            v = t[:, :].rearrange("p (i n) -> p i n", i=4)
            if g % 2:
                q.do(lambda e: e.copy(qc[c % 2][:, :, g, :], v), s)
            else:
                q.do(lambda e: e.tensor_copy(qc[c % 2][:, :, g, :], v), s)
            done[("qc", c, g)] = (s, sems.count[s])

        def KCOMB(c, g):
            pe.wait("c_sel", 4)
            pe.wait("kl", c + 1)
            t, s = misc.take(pe)
            pe.do(lambda e: e.matmul(t[:, 0:KC], selr[:, 8 + g, :], kh[:, :], start=True, stop=False))
            pe.do(lambda e: e.matmul(t[:, 0:KC], selr[:, 12 + g, :], kl[:, :], start=False, stop=True), "kc")
            act.wait("kc", 4 * c + g + 1)
            if c >= 2:
                act.wait("T", 16 * (c - 1))
                for p in (2 * c - 4, 2 * c - 3):
                    act.wait(f"kd{p % 2}", 64 * (p // 2 + 1))
            act.do(lambda e: e.activation(kc[c % 2][:, :, g, :], t[:, 0:KC].rearrange("p (i n) -> p i n", i=4), ACT.Identity,
                                          bias=cols[:, 4:5]), s)
            done[("kc", c, g)] = (s, sems.count[s])

        def VP(c):
            pe.wait("ld_w", n_ldw)
            t, s = misc.take(pe)
            for i in range(4):
                pe.do(lambda e, i=i: e.matmul(t[0:CS, i * 128:(i + 1) * 128], cf[c % 2][:, i * CS:(i + 1) * CS], vwf[:, :],
                                              start=True, stop=True), "v" if i == 3 else None)
            dve.wait("v", c + 1)
            dve.wait("c_v9", 2)
            if c >= 2:
                dve.wait("Og", 16 * (c - 1))
            for i in range(4):
                dve.do(lambda e, i=i: e.tensor_tensor(v9[c % 2][:, i * H:(i + 1) * H, 0:8],
                                                      t[0:CS, i * 128:(i + 1) * 128].rearrange("p (h d) -> p h d", h=H),
                                                      vbb[:, :].rearrange("p (h d) -> p h d", h=H), ALU.add),
                       s if i == 3 else "v9")
            done[("v", c)] = (s, sems.count[s])

        def KD(p):
            c, i, s = p // 2, 2 * (p % 2), p % 2
            for g in range(4):
                sp.wait(*done[("kc", c, g)])
            sp.wait("c_kd", 2)
            if p >= 2:
                sp.wait("S", 8 * (p - 1))
            for j in range(4):
                load(kd[s][32 * j:32 * j + 32, :, :, j, :].rearrange("p i g m -> p (i g) m").bitcast(F),
                     kc[c % 2][32 * j:32 * j + 32, i:i + 2, :, :].rearrange("p i g m -> p (i g) m").bitcast(F), f"kd{s}")

        def QD(p):
            c, i, s = p // 2, 2 * (p % 2), p % 2
            for g in range(4):
                sp.wait(*done[("qc", c, g)])
            sp.wait("c_qd", 2)
            if p >= 2:
                sp.wait("T", 8 * (p - 1))
            for j in range(4):
                load(qd[s][32 * j:32 * j + 32, :, :, j, :].rearrange("p i g m -> p (i g) m").bitcast(F),
                     qc[c % 2][32 * j:32 * j + 32, i:i + 2, :, :].rearrange("p i g m -> p (i g) m").bitcast(F), f"qd{s}")

        def SC(b, g):
            c, i, p = b // 4, b % 4, b // 2
            pe.wait(*done[("qc", c, g)])
            pe.wait(f"kd{p % 2}", 64 * (p // 2 + 1))
            t, f = bS.take(pe)
            pe.do(lambda e: e.matmul(t[:, 0:KC], qc[c % 2][:, i, g, :], kd[p % 2][:, b % 2, g, :, :], start=True, stop=True), "S")
            dve.wait("S", 4 * b + g + 1)
            if b >= 2:
                dve.wait("mT", b - 1)
            dve.do(lambda e: e.tensor_reduce(mx[b % 2][:, 4 * g:4 * g + 4], t[:, 0:KC].rearrange("p (j m) -> p j m", j=4),
                                             AX.X, ALU.max, negate=True), f)
            done[("mx", b, g)] = (f, sems.count[f])

        def MT(b):
            p = b // 2
            for g in range(4):
                pe.wait(*done[("mx", b, g)])
            t, f = misc.take(pe)
            pe.do(lambda e: e.transpose(t[0:16, 0:128], mx[b % 2][:, :], idf[:, :]), "mT")
            act.wait("mT", b + 1)
            if b >= 2:
                act.wait(f"nm{b % 2}", 16 * (b // 2))
            act.do(lambda e: e.copy(nm[b % 2][:, :], t[0:16, 0:128]), f)
            sp.wait(f, sems.count[f])
            sp.wait(f"qd{p % 2}", 64 * (p // 2 + 1))
            load(qd[p % 2][24:25, b % 2, :, :, :].rearrange("p g j n -> p (g j) n").bitcast(F), nm[b % 2][:, :].bitcast(F), f"nm{b % 2}")

        def ST(b, g):
            c, i, p, k = b // 4, b % 4, b // 2, 4 * b + g
            pe.wait(f"nm{b % 2}", 16 * (b // 2 + 1))
            t, f = bT.take(pe)
            pe.do(lambda e: e.matmul(t[0:CS, :], kc[c % 2][:, i, g, :], qd[p % 2][:, b % 2, g, :, :], start=True, stop=True), "T")
            act.wait("T", k + 1)
            if k >= 4:
                act.wait("Og", k - 3)
            act.do(lambda e: e.activation(P[k % 4][:, :], t[0:CS, :], ACT.Exp), f)
            done[("p", b, g)] = (f, sems.count[f])

        def PV(b, g):
            c, i, k = b // 4, b % 4, 4 * b + g
            pe.wait(*done[("v", c)])
            pe.wait("c_o", 1)
            pe.wait(*done[("p", b, g)])
            if g == 0:
                PV.t, PV.f = bO.take(pe)
            t, f = PV.t, PV.f
            for j in range(4):
                pe.do(lambda e, j=j: e.matmul(t[32 * j:32 * j + 9, g * 128:(g + 1) * 128], v9[c % 2][:, i * H + 4 * g + j, :],
                                              P[k % 4][:, j * S:(j + 1) * S], start=True, stop=True),
                      "Og" if j == 3 else None)
            if g == 3:
                act.wait("Og", k + 1)
                if b >= 2:
                    act.wait("oX", b - 1)
                act.wait("c_z", 2)
                act.do(lambda e: e.copy(osb[b % 2][:, :, :], t[:, :]), f)
                done[("osb", b)] = (f, sems.count[f])

        def OT(b):
            pe.wait(*done[("osb", b)])
            t, f = misc.take(pe)
            for g in range(4):
                pe.do(lambda e, g=g: e.transpose(t[:, g * 128:(g + 1) * 128], osb[b % 2][:, g, :], idf[:, :]),
                      "oX" if g == 3 else None)
            v = t[:, :].rearrange("p (h r) -> p h r", r=32)
            dve.wait("oX", b + 1)
            if b >= 2:
                dve.wait(done[("on", b - 2)][0], done[("on", b - 2)][1])
            dve.do(lambda e: e.reciprocal(rd[b % 2][:, :], v[:, :, 8]), "rd")
            dve.wait("rd", b + 1)
            if b >= 2:
                dve.wait("onT", b - 1)
            dve.do(lambda e: e.tensor_tensor(on[b % 2][:, :].rearrange("p (h d) -> p h d", d=8), v[:, :, 0:8],
                                             rd[b % 2][:, :].unsqueeze(2).to_broadcast([128, 16, 8]), ALU.mult), f)
            done[("on", b)] = (f, sems.count[f])

        def ONT(b):
            pe.wait(*done[("on", b)])
            t, f = misc.take(pe)
            pe.do(lambda e: e.transpose(t[:, 0:128], on[b % 2][:, :], idf[:, :]), "onT")
            act.wait("onT", b + 1)
            if b >= 2:
                act.wait("pr", b - 1)
            act.do(lambda e: e.copy(oT[b % 2][:, :], t[:, 0:128]), f)
            done[("oT", b)] = (f, sems.count[f])

        def PR(b):
            c, i = b // 4, b % 4
            pe.wait(*done[("oT", b)])
            t, f = misc.take(pe)
            pe.do(lambda e: e.matmul(t[:, 0:128], oT[b % 2][:, :], pwf[:, :], start=True, stop=True), "pr")
            dve.wait("pr", b + 1)
            dve.wait("xp", 4 * c + 4)
            if c >= 3:
                dve.wait("xr", 4 * (c - 2))
            dve.do(lambda e: e.tensor_tensor(x1[c % 3][:, i, :], t[:, 0:128], xin[c % 4][:, i, :], ALU.add), f)
            done[("x1", b)] = (f, sems.count[f])

        def N2(c):
            steps = norm_stats(c, 1, x1[c % 3])

            def first():
                for b in range(4 * c, 4 * c + 4):
                    dve.wait(*done[("x1", b)])
                steps[0]()

            def apply():
                pool.wait("c_lo", 3)
                if c >= 2:
                    pool.wait("xr", 4 * (c - 1))
                    pool.wait("bst2", 4 * (c - 1))
                norm_apply(c, 1, hh[c % 2], x1[c % 3], "hh")

            return [first] + steps[1:] + [None] * 5 + [apply]

        def XR(c):
            pool.wait("hh", 4 * c + 4)
            if c >= 2:
                pool.wait(f"sx{c % 2}", 16 * (c // 2))
            for i in range(4):
                pool.do(lambda e, i=i: e.tensor_tensor(xr[c % 2][:, i, :], x1[c % 3][:, i, :], hh[c % 2][:, i, :], ALU.add), "xr")
            sp.wait("xr", 4 * c + 4)
            load(xres[c], xr[c % 2][:, :, :].rearrange("p a b -> p (a b)"), f"sx{c % 2}")

        def N3(c):
            steps = norm_stats(c, 2, hh[c % 2])

            def apply():
                pool.wait("c_sel", 4)
                if c >= 2:
                    pool.wait("zT", c - 1)
                norm_apply(c, 2, zz[c % 2], hh[c % 2], "zz")

            return [lambda: dve.wait("hh", 4 * c + 4) or steps[0]()] + steps[1:] + [None] * 5 + [apply]

        def ZT(c):
            pe.wait("zz", 4 * c + 4)
            t, f = misc.take(pe)
            for i in range(4):
                pe.do(lambda e, i=i: e.transpose(t[:, i * 128:(i + 1) * 128], zz[c % 2][:, i, :], idf[:, :]),
                      "zT" if i == 3 else None)
            act.wait("zT", c + 1)
            act.do(lambda e: e.activation(xnT[:, c * TC:(c + 1) * TC], t[:, :], ACT.Identity, bias=cols[:, 3:4],
                                          scale=cols[:, 2:3]), f)
            done[("xn", c)] = (f, sems.count[f])

        def ZH(c):
            dve.wait(*done[("xn", c)])
            dve.wait("rt", c)
            dve.do(lambda e: e.tensor_copy(zh[:, :], xnT[:, c * TC:(c + 1) * TC]), "zh")

        def ZL(c):
            dve.wait("zh", c + 1)
            dve.do(lambda e: e.tensor_tensor(zl[:, :], xnT[:, c * TC:(c + 1) * TC], zh[:, :].bitcast(F), ALU.subtract), "zl")

        def RT(c):
            pe.wait("zl", c + 1)
            t, f = misc.take(pe)
            three(pe, t[:, :], (rwh[:, :], rwl[:, :]), (zh[:, :], zl[:, :]), "rt")
            act.wait("rt", c + 1)
            act.wait("lT", c)
            act.do(lambda e: e.copy(lg[:, :], t[0:8, :]), f)
            done[("lg", c)] = (f, sems.count[f])

        def LT(c):
            b = c % 2
            pe.wait(*done[("lg", c)])
            t, f = misc.take(pe)
            for i in range(4):
                pe.do(lambda e, i=i: e.transpose(t[:, i * 8:(i + 1) * 8], lg[:, i * 128:(i + 1) * 128], idf[0:8, 0:8]),
                      "lT" if i == 3 else None)
            v = t[:, 0:32].rearrange("p (i e) -> p i e", e=8)
            dve.wait("lT", c + 1)
            dve.do(lambda e: e.tensor_reduce(s4[b][:, 0, :], v, AX.X, ALU.max), "r1")
            done[("lgt", c)] = (v, f)

        def LS(c):
            b = c % 2
            v, f = done[("lgt", c)]
            dve.wait("r1", c + 1)
            dve.do(lambda e: e.tensor_tensor(sm[b][:, 0, :, :], v, s4[b][:, 0, :].unsqueeze(2).to_broadcast([128, 4, 8]),
                                             ALU.subtract), f)
            act.wait(f, sems.count[f])
            act.do(lambda e: e.activation(sm[b][:, 1, :, :], sm[b][:, 0, :, :], ACT.Exp, scale=1.0 / TEMP), "r2")

        def TOP(c):
            b = c % 2
            s_, r_ = sm[b], s4[b]

            def total():
                dve.wait("r2", c + 1)
                dve.do(lambda e: e.tensor_reduce(r_[:, 1, :], s_[:, 1, :, :], AX.X, ALU.add), "r3")

            def inverse():
                dve.wait("r3", c + 1)
                dve.do(lambda e: e.reciprocal(r_[:, 2, :], r_[:, 1, :]), "r4")

            def probs():
                dve.wait("r4", c + 1)
                dve.do(lambda e: e.tensor_tensor(s_[:, 2, :, :], s_[:, 1, :, :],
                                                 r_[:, 2, :].unsqueeze(2).to_broadcast([128, 4, 8]), ALU.mult), "r5")

            def sort(*i4):
                dve.wait("r5", c + 1)
                for i in i4:
                    dve.do(lambda e, i=i: e.max(m8[b][:, i, :], s_[:, 2, i, :]), "r6")

            def index(*i4):
                dve.wait("r6", 4 * c + 4)
                for i in i4:
                    dve.do(lambda e, i=i: e.max_index(i8[b][:, i, :], m8[b][:, i, :], s_[:, 2, i, :]), "r7")

            def floats():
                dve.wait("r7", 4 * c + 4)
                dve.do(lambda e: e.tensor_copy(if8[b][:, :, :], i8[b][:, :, :]), "r8")

            def equal():
                dve.wait("r8", c + 1)
                for k in range(2):
                    dve.do(lambda e, k=k: e.tensor_tensor(s_[:, 3 * k, :, :], iot[:, :, :],
                                                          if8[b][:, :, k].unsqueeze(2).to_broadcast([128, 4, 8]),
                                                          ALU.is_equal), "r9")

            def either():
                dve.wait("r9", 2 * c + 2)
                dve.do(lambda e: e.tensor_tensor(s_[:, 0, :, :], s_[:, 0, :, :], s_[:, 3, :, :], ALU.add), "r10")

            def weights():
                dve.wait("r10", c + 1)
                if c >= 2:
                    dve.wait("wT", c - 1)
                dve.do(lambda e: e.tensor_tensor(wd[b][:, :, :], s_[:, 0, :, :], s_[:, 2, :, :], ALU.mult), "wd")

            return [total, inverse, probs, lambda: sort(0, 1), lambda: sort(2, 3), lambda: index(0, 1), lambda: index(2, 3), floats, equal, either, weights]

        def WT(c):
            b = c % 2
            pe.wait("wd", c + 1)
            t, f = misc.take(pe)
            pe.do(lambda e: e.transpose(t[0:32, 0:128], wd[b][:, :, :].rearrange("p a b -> p (a b)"), idf[:, :]), "wT")
            act.wait("wT", c + 1)
            if c >= 2:
                act.wait(f"sw{b}", 16 * (c // 2))
            act.do(lambda e: e.copy(wts[b][:, :], t[0:32, 0:128]), f)
            sp.wait(f, sems.count[f])
            load(wsc[c], wts[b][:, :], f"sw{b}")

        def at(c, *fns):
            return [lambda fn=fn: fn(c) for fn in fns] if 0 <= c < NC else []

        def front(c0, i):
            c, n = c0 + 1, c0 + 2
            if i == 0:
                return at(c, CT, XH, CH, CL, XT, XP)
            if i == 1:
                return at(c, KP, QP, KH) + at(n, LX) + at(c, KL, QH, QL) + [None]
            two = lambda *gs: [(lambda g=g: KCOMB(c, g)) if k == "k" else (lambda g=g: QC(c, g)) for k, g in gs] if 0 <= c < NC else []
            if i == 2:
                return two(("k", 0), ("k", 1), ("k", 2), ("k", 3), ("q", 0), ("q", 1))
            return two(("q", 2), ("q", 3)) + at(c, VP) + (LN1(n) if 0 <= n < NC else [])

        def after(c):
            gap = lambda n: [None] * n
            return (N2(c) + gap(7) + N3(c) + at(c, XR) + gap(8) + at(c, ZT) + gap(3) + at(c, ZH, ZL) + gap(3) + at(c, RT)
                    + gap(4) + [lambda: LT(c) or LS(c)] + gap(3) + TOP(c) + gap(2) + at(c, WT))

        tail = []
        ok = lambda b: 0 <= b < NB
        for t in range(-8, NB + 15):
            c0, i = divmod(t, 4)
            if i == 1 and 0 <= c0 - 2 < NC:
                tail += after(c0 - 2)
            near = front(c0, i)
            steps = []
            if t % 2 == 1 and ok(t + 1):
                KD((t + 1) // 2)
            if t % 2 == 0 and ok(t):
                steps.append(lambda: QD(t // 2))
            u, v = t - 2, t - 3
            for g in range(4):
                if ok(t):
                    steps.append(lambda g=g: SC(t, g))
                if ok(u):
                    steps.append(lambda g=g: ST(u, g))
                if g < 2 and ok(v):
                    steps.append(lambda g=g: PV(v, g + 2))
                if g >= 2 and ok(u):
                    steps.append(lambda g=g: PV(u, g - 2))
                if g == 0 and ok(t - 4):
                    steps.append(lambda: ONT(t - 4))
                if g == 1 and ok(t - 1):
                    steps.append(lambda: MT(t - 1))
                if g == 2 and ok(t - 4):
                    steps.append(lambda: PR(t - 4))
                if g == 2 and ok(v):
                    steps.append(lambda: OT(v))
            n = max(len(steps), 1)
            fed = 0
            for k in range(n):
                if k < len(steps):
                    steps[k]()
                while near and fed < len(near) * (k + 1) // n:
                    f_ = near[fed]
                    fed += 1
                    if f_:
                        f_()
                if tail:
                    f_ = tail.pop(0)
                    if f_:
                        f_()
            for f_ in near[fed:]:
                if f_:
                    f_()
        for f_ in tail:
            if f_:
                f_()

        endA = {k: v for k, v in sems.count.items() if v}
        sa.close()
        pa.close()

        sb_, pb_ = ExitStack(), ExitStack()
        nb = [0]

        def Bt(shape, dt=F, n=1):
            nb[0] += 1
            ts = [sbt(sb_, f"b{nb[0]}_{i}", shape, dt) for i in range(n)]
            return ts[0] if n == 1 else ts

        w1h, w1l, w2h, w2l = (Bt([128, E, 512], R) for _ in range(4))
        wraw = Bt([128, 2, 512], F, 2)
        gh, gl = Bt([128, TC], R, 2), Bt([128, TC], R, 2)
        sf, sh, sl = Bt([128, TC], F, 3), Bt([128, TC], R, 6), Bt([128, TC], R, 6)
        wb = Bt([128, TC], F, 4)
        ty = Bt([128, TC], F, 2)
        acc = Bt([128, TC], F, 2)
        xo = Bt([128, TC], F, 2)
        oo = Bt([128, TC], F, 2)
        bH, bY, bF = Banks("bH", pt(pb_, "qh", 4)), InOrder("yw", pt(pb_, "qy", 2)), InOrder("oo", pt(pb_, "qf", 1))

        for q in (pe, act, dve, sp):
            for k, v in endA.items():
                q.wait(k, v)

        W2v = W2.rearrange("e (k p) d -> e p k d", p=128)

        def WL(e_):
            s = e_ % 2
            if e_ >= 2:
                sp.wait("wlo", 2 * (e_ - 1))
            load(wraw[s][:, 0, :], W1[e_], f"wr{s}")
            load(wraw[s][:, 1, :].rearrange("p (k d) -> p k d", k=4), W2v[e_], f"wr{s}")

        def WS(e_):
            s = e_ % 2
            dve.wait(f"wr{s}", 32 * (e_ // 2 + 1))
            for hi, k in ((w1h, 0), (w2h, 1)):
                dve.do(lambda e, hi=hi, k=k: e.tensor_copy(hi[:, e_, :], wraw[s][:, k, :]), "whi")
            dve.wait("whi", 2 * e_ + 2)
            for hi, lo, k in ((w1h, w1l, 0), (w2h, w2l, 1)):
                dve.do(lambda e, hi=hi, lo=lo, k=k: e.tensor_tensor(lo[:, e_, :], wraw[s][:, k, :], hi[:, e_, :].bitcast(F),
                                                                  ALU.subtract), "wlo")

        def GP(c):
            s = c % 2
            if c >= 2:
                dve.wait("M1", 32 * (c - 1))
            dve.do(lambda e: e.tensor_copy(gh[s][:, :], xnT[:, c * TC:(c + 1) * TC]), "gh")
            dve.wait("gh", c + 1)
            dve.do(lambda e: e.tensor_tensor(gl[s][:, :], xnT[:, c * TC:(c + 1) * TC], gh[s][:, :].bitcast(F), ALU.subtract), "gl")

        def WB(u):
            c, e_, s = u // E, u % E, u % 4
            if u >= 4:
                sp.wait("yw", u - 3)
            src = wsc[c].rearrange("(t e) n -> e t n", t=4)[e_].partition_broadcast(128)
            load(wb[s][:, :].rearrange("p (t n) -> p t n", t=4), src, f"wb{s}")

        def M1(u, f):
            c, e_, k = u // E, u % E, 4 * u + f
            pe.wait("wlo", 2 * min(u + 1, E))
            pe.wait("gl", c + 1)
            t, s = bH.take(pe)
            fs = slice(f * 128, (f + 1) * 128)
            three(pe, t[:, :], (w1h[:, e_, fs], w1l[:, e_, fs]), (gh[c % 2][:, :], gl[c % 2][:, :]), "M1")
            act.wait("M1", k + 1)
            if k >= 3:
                act.wait("sl", k - 2)
            act.do(lambda e: e.activation(sf[k % 3][:, :], t[:, :], ACT.Silu), "sf")
            if k >= 6:
                act.wait("M2", k - 5)
            act.do(lambda e: e.activation(sh[k % 6][:, :], t[:, :], ACT.Silu), s)
            dve.wait("sf", k + 1)
            dve.wait(s, sems.count[s])
            if k >= 6:
                dve.wait("M2", k - 5)
            dve.do(lambda e: e.tensor_tensor(sl[k % 6][:, :], sf[k % 3][:, :], sh[k % 6][:, :].bitcast(F), ALU.subtract), "sl")

        def M2(u, f):
            c, e_, k = u // E, u % E, 4 * u + f
            pe.wait("sl", k + 1)
            if f == 0:
                M2.t, _ = bY.take(pe)
            t = M2.t
            fs = slice(f * 128, (f + 1) * 128)
            pe.do(lambda e: e.matmul(t[:, :], w2l[:, e_, fs], sh[k % 6][:, :], start=(f == 0), stop=False))
            pe.do(lambda e: e.matmul(t[:, :], w2h[:, e_, fs], sh[k % 6][:, :], start=False, stop=False))
            pe.do(lambda e: e.matmul(t[:, :], w2h[:, e_, fs], sl[k % 6][:, :], start=False, stop=(f == 3)), "M2")

        def YW(u):
            c, e_, s = u // E, u % E, u % 4
            t = M2.t
            dve.wait("M2", 4 * u + 4)
            dve.wait(f"wb{s}", 16 * (u // 4 + 1))
            if e_ == 0:
                if c >= 2:
                    dve.wait("fT", c - 1)
                dve.do(lambda e: e.tensor_tensor(acc[c % 2][:, :], t[:, :], wb[s][:, :], ALU.mult), "yw")
            else:
                dve.do(lambda e: e.tensor_tensor(ty[u % 2][:, :], t[:, :], wb[s][:, :], ALU.mult), "yw")
            dve.wait("yw", u + 1)
            if e_:
                if e_ > 1:
                    dve.wait("ac", c * 7 + e_ - 1)
                dve.do(lambda e: e.tensor_tensor(acc[c % 2][:, :], acc[c % 2][:, :], ty[u % 2][:, :], ALU.add), "ac")

        def XO(c):
            s = c % 2
            if c >= 2:
                sp.wait("oo", c - 1)
            load(xo[s][:, :], xres[c], f"xo{s}")

        def FIN(c):
            s = c % 2
            pe.wait("ac", 7 * c + 7)
            t, f = bF.take(pe)
            for i in range(4):
                pe.do(lambda e, i=i: e.transpose(t[:, i * 128:(i + 1) * 128], acc[s][:, i * 128:(i + 1) * 128], idf[:, :]),
                      "fT" if i == 3 else None)
            dve.wait("fT", c + 1)
            dve.wait(f"xo{s}", 16 * (c // 2 + 1))
            if c >= 2:
                dve.wait(f"so{s}", 16 * (c // 2))
            dve.do(lambda e: e.tensor_tensor(oo[s][:, :], t[:, :], xo[s][:, :], ALU.add), "oo")
            sp.wait("oo", c + 1)
            load(out[4 * c:4 * c + 4].rearrange("b n d -> n b d"), oo[s][:, :].rearrange("p (b d) -> p b d", b=4), f"so{s}")

        WL(0)
        WL(1)
        WB(0)
        WB(1)
        GP(0)
        NU = NC * E
        LAG = 3
        for k in range(4 * NU + LAG + 1):
            u, f = divmod(k, 4)
            c, e_ = divmod(u, E)
            if u < NU:
                if f == 0:
                    if u < E:
                        WS(u)
                        if u + 2 < E:
                            WL(u + 2)
                    if u + 2 < NU:
                        WB(u + 2)
                    if e_ == 4:
                        XO(c)
                        if c + 1 < NC:
                            GP(c + 1)
                M1(u, f)
            k2 = k - LAG
            if 0 <= k2 < 4 * NU:
                u2, f2 = divmod(k2, 4)
                M2(u2, f2)
                if f2 == 3:
                    YW(u2)
            if k >= 4 * E and (k - 4 * E) % (4 * E) == 6:
                FIN((k - 4 * E) // (4 * E))
        FIN(NC - 1)
        for s in range(2):
            sp.wait(f"so{s}", 16 * (NC // 2))
            sp.wait(f"sx{s}", 16 * (NC // 2))
            sp.wait(f"sw{s}", 16 * (NC // 2))

        block = st.enter_context(nc.Block())

        @block.sync
        def _(e):
            sp.emit(e)

        @block.tensor
        def _(e):
            pe.emit(e)

        @block.scalar
        def _(e):
            act.emit(e)

        @block.vector
        def _(e):
            dve.emit(e)

        @block.gpsimd
        def _(e):
            pool.emit(e)

        pb_.close()
        sb_.close()


def _selectors():
    import numpy as np
    sel = np.zeros((128, 16, 128), np.float32)
    for kind, parts in enumerate(((0, 2), (1,), (0, 1), (2,))):
        for g in range(4):
            for j in range(4):
                for d in range(HD):
                    for p in parts:
                        sel[(4 * g + j) * HD + d, 4 * kind + g, 32 * j + 8 * p + d] = 1.0
    return sel


def kernel(**inputs):
    import numpy as np
    import concourse.bacc as bacc
    from concourse.bass_utils import run_bass_kernel_spmd

    i = {k: np.asarray(v) for k, v in inputs.items()}
    col = lambda a: a.reshape(128, 1)
    rows = lambda a, n: np.broadcast_to(a.reshape(1, 128), (n, 128))
    one24 = np.zeros((128, 1), np.float32)
    one24[24] = 1.0
    iota = np.broadcast_to(np.arange(8, dtype=np.float32), (128, 4, 8))
    args = [
        ("x", i["x"]), ("ctx", i["ctx_768"]), ("qw", i["L0_xattn_q_w"]), ("qb", col(i["L0_xattn_q_b"])),
        ("kw", i["L0_xattn_kv_w"][:, 0:128]), ("kb", col(i["L0_xattn_kv_b"][0:128])),
        ("vw", i["L0_xattn_kv_w"][:, 128:256]), ("vb", rows(i["L0_xattn_kv_b"][128:256], CS)),
        ("pw", i["L0_xattn_proj_w"]), ("pb", rows(i["L0_xattn_proj_b"], 128)),
        ("gam", col(i["L0_ffn_gamma"])), ("bet", col(i["L0_ffn_beta"])), ("rwT", i["L0_ffn_router_w"].T),
        ("W1", i["L0_ffn_W1"]), ("W2", i["L0_ffn_W2"]), ("ident", np.eye(128, dtype=np.float32)),
        ("sel", _selectors()), ("one24", one24), ("iota", iota),
    ]
    nc = bacc.Bacc("TRN2", target_bir_lowering=False, num_devices=1)
    arrays, aps = {}, []
    for name, a in args:
        a = np.ascontiguousarray(a)
        arrays[f"in_{name}"] = a
        aps.append(nc.dram_tensor(f"in_{name}", a.shape, mybir.dt.from_np(a.dtype), kind="ExternalInput").ap())
    o = nc.dram_tensor("out_0", (NB, S, D), F, kind="ExternalOutput").ap()
    xattn_moe(nc, *aps, o)
    r = run_bass_kernel_spmd(nc, [arrays], core_ids=[0])
    return r.results[0]["out_0"]
```

```python
from contextlib import ExitStack

import concourse.bass as bass
from concourse import mybir

F = mybir.dt.float32
R = mybir.dt.float32r
U32 = mybir.dt.uint32
ALU = mybir.AluOpType
ACT = mybir.ActivationFunctionType
AX = mybir.AxisListType

NB, S, D = 64, 128, 128
CS, CD = 77, 96
H, HD = 16, 8
E, FF = 8, 512
NC = NB // 4
TC = 4 * S
KC = 4 * CS
SCALE = float(HD) ** -0.5
EPS = 1e-5
TEMP = 1.5


ORDER = "SC0 Pv2 ST0 ON SC1 Pv3 ST1 MT SC2 ST2 PR Pu0 OT SC3 ST3 Pu1"


class Queue:

    def __init__(self, sems):
        self.items, self.sems, self.seen = [], sems, {}

    def wait(self, name, value):
        if value > self.seen.get(name, 0):
            self.seen[name] = value
            self.items.append((name, value))

    def do(self, fn, sem=None, n=1):
        self.items.append((fn, sem, n))
        if sem is not None:
            self.sems.count[sem] = self.sems.count.get(sem, 0) + n

    def emit(self, eng):
        for it in self.items:
            if isinstance(it[0], str):
                eng.wait_ge(self.sems[it[0]], it[1])
            else:
                ins = it[0](eng)
                if it[1] is not None:
                    ins.then_inc(self.sems[it[1]], it[2])


class Sems:

    def __init__(self, nc, ctx):
        self.nc, self.ctx, self.count, self.made = nc, ctx, {}, {}

    def __getitem__(self, name):
        if name not in self.made:
            self.made[name] = self.ctx.enter_context(self.nc.semaphore("s_" + name))
        return self.made[name]


class Banks:

    def __init__(self, name, tiles):
        self.name, self.tiles, self.n = name, tiles, 0
        self.turn, self.uses = list(range(len(tiles))), [0] * len(tiles)

    def free(self, q, slot):
        q.wait(f"{self.name}{slot}", self.uses[slot])

    def take(self, q):
        slot = self.turn[self.n % len(self.turn)]
        self.n += 1
        self.free(q, slot)
        self.uses[slot] += 1
        return self.tiles[slot], f"{self.name}{slot}"


class InOrder(Banks):

    def take(self, q):
        k = self.n
        self.n += 1
        q.wait(self.name, k - len(self.tiles) + 1)
        return self.tiles[k % len(self.tiles)], self.name


def xattn_moe(nc, x, ctx_in, qw, qb, kw, kb, vw, vb, pw, pb, gam, bet, rwT, W1, W2, ident, sel, one24, iota, out):
    st = ExitStack()
    with st:
        sems = Sems(nc, st)
        pe, act, dve, pool, sp = (Queue(sems) for _ in range(5))

        def sbt(ctx, name, shape, dt=F):
            return ctx.enter_context(nc.sbuf_tensor(name, shape, dt))

        xres = nc.dram_tensor("xres", (NC, 128, 512), F, kind="Internal").ap()
        wsc = nc.dram_tensor("wsc", (NC, 32, 128), F, kind="Internal").ap()

        xnT = sbt(st, "xnT", [128, NC * TC])
        idf = sbt(st, "idf", [128, 128])

        sa = ExitStack()
        nm_ = [0]

        def A(shape, dt=F, n=1):
            nm_[0] += 1
            ts = [sbt(sa, f"a{nm_[0]}_{i}", shape, dt) for i in range(n)]
            return ts[0] if n == 1 else ts

        def K(shape, dt=F, n=1):
            nm_[0] += 1
            ts = [sbt(st, f"k{nm_[0]}_{i}", shape, dt) for i in range(n)]
            return ts[0] if n == 1 else ts

        selr = K([128, 16, 128], R)
        rwh, rwl = (K([128, 128], R) for _ in range(2))
        cols = K([128, 8])
        iot = K([128, 4, 8])
        nhalf = K([128, 4])
        xh = K([128, 4, 128], F, 2)
        xTh = K([128, TC], R)
        xTl = K([128, TC], R)
        x1 = K([128, 4, 128], F, 3)
        hh = K([128, 4, 128], F, 2)
        zz = K([128, 4, 128], F, 2)
        xr = K([128, 4, 128], F, 2)
        bst = K([128, 3, 4, 6])
        mv = K([128, 3, 4, 2], F, 2)
        rs = K([128, 3, 4], F, 2)
        ve = K([128, 3, 4], F, 2)
        ng = K([128, 3, 4], F, 2)
        zh, zl = K([128, TC], R), K([128, TC], R)
        lg = K([8, TC])
        sm = K([128, 4, 4, 8], F, 2)
        s4 = K([128, 3, 4], F, 2)
        m8 = K([128, 4, 8], F, 2)
        i8 = K([128, 4, 8], U32, 2)
        if8 = K([128, 4, 8], F, 2)
        wd = K([128, 4, 8], F, 2)
        wts = K([32, 128], F, 2)
        stg, wst = zz, hh[0]

        qwh, qwl = (A([128, 128], R) for _ in range(2))
        kwh, kwl = (A([CD, 128], R) for _ in range(2))
        vwf = A([CD, 128])
        pwf = A([128, 128])
        vbb = A([CS, 128])
        pbb = A([128, 128])
        xin = A([128, 4, 128], F, 4)
        cin = A([CS, 4, CD], F, 3)
        cf = A([CD, KC], F, 2)
        ch, cl = A([CD, KC], R), A([CD, KC], R)
        qf = A([128, TC])
        qh, ql = A([128, TC], R), A([128, TC], R)
        kf = A([128, KC])
        kh, kl = A([128, KC], R), A([128, KC], R)
        qc = A([128, 4, 4, S], R, 2)
        kc = A([128, 4, 4, CS], R, 2)
        qd = A([128, 2, 4, 4, S], R, 2)
        kd = A([128, 2, 4, 4, CS], R, 2)
        v9 = A([CS, 4 * H, 9], F, 2)
        P = A([CS, 4 * S], F, 4)
        mx = A([128, 16], F, 2)
        nm = A([16, 128], R, 2)
        osb = A([128, 4, 128], F, 2)
        rd = A([128, 16], F, 2)
        on = A([128, 128], F, 2)
        oT = A([128, 128], F, 2)

        def pt(ctx, name, n):
            return [ctx.enter_context(nc.psum_tensor(f"{name}{i}", [128, 512], F)) for i in range(n)]

        misc, bS, bT = Banks("misc", pt(st, "pm", 3)), Banks("bS", pt(st, "ps", 2)), Banks("bT", pt(st, "pt", 2))
        bO = Banks("bO", pt(st, "po", 1))

        def load(dst, src, sem):
            sp.do(lambda e: e.dma_start(dst, src), sem, 16)

        def x_load(c):
            load(xin[c % 4][:, :, :], x[4 * c:4 * c + 4].rearrange("b n d -> n b d"), f"lx{c % 4}")

        def c_load(c):
            load(cin[c % 3][:, :, :], ctx_in[4 * c:4 * c + 4].rearrange("b m d -> m b d"), f"lc{c % 3}")

        x_load(0)
        load(idf[:, :], ident, "ld_id")
        c_load(0)
        for dst, src in ((wst[:, 0, :], qw), (wst[0:CD, 1, :], kw), (wst[:, 2, 0:8], rwT), (cols[:, 0:1], qb),
                         (cols[:, 1:2], kb), (cols[:, 4:5], one24)):
            load(dst, src, "ld_w")
        for g in range(2):
            load(stg[g][:, :, :], sel[:, 8 + 4 * g:12 + 4 * g, :], f"ld_sel{g}")
        for dst, src in ((vwf[:, :], vw), (pwf[:, :], pw), (vbb[:, :], vb), (pbb[:, :], pb), (cols[:, 2:3], gam),
                         (cols[:, 3:4], bet), (iot[:, :, :], iota)):
            load(dst, src, "ld_v")
        n_ldw, n_ldv = sems.count["ld_w"], sems.count["ld_v"]

        dve.do(lambda e: e.memset(bO.tiles[0][:, :], 0.0), "c_o")
        dve.do(lambda e: e.memset(nhalf[:, :], -0.5), "c_nh")
        for i in range(2):
            dve.do(lambda e, i=i: e.memset(v9[i][:, :, :], 1.0), "c_v9")
            dve.do(lambda e, i=i: e.memset(osb[i][:, :, :], 0.0), "c_z")

        def clear(i):
            pool.do(lambda e: e.memset(kd[i][:, :, :, :, :].bitcast(F), 0.0), "c_kd")
            pool.do(lambda e: e.memset(qd[i][:, :, :, :, :].bitcast(F), 0.0), "c_qd")

        clear(0)
        def weights_prep():
            dve.do(lambda e: e.memset(rwh[:, :].bitcast(F), 0.0), "c_rw")
            dve.do(lambda e: e.memset(rwl[:, :].bitcast(F), 0.0), "c_rw")
            dve.wait("ld_w", n_ldw)
            dve.wait("c_rw", 2)
            dve.do(lambda e: e.tensor_scalar(cols[:, 0:1], cols[:, 0:1], SCALE, None, ALU.mult), "c_qb")
            for hi, src, k in ((qwh[:, :], wst[:, 0, :], "qw"), (kwh[:, :], wst[0:CD, 1, :], "kw"), (rwh[:, 0:8], wst[:, 2, 0:8], "rw")):
                dve.do(lambda e, hi=hi, src=src: e.tensor_copy(hi, src), "c_hi")
            dve.wait("c_hi", 3)
            for hi, lo, src in ((qwh[:, :], qwl[:, :], wst[:, 0, :]), (kwh[:, :], kwl[:, :], wst[0:CD, 1, :]),
                                (rwh[:, 0:8], rwl[:, 0:8], wst[:, 2, 0:8])):
                dve.do(lambda e, hi=hi, lo=lo, src=src: e.tensor_tensor(lo, src, hi.bitcast(F), ALU.subtract), "c_lo")

        def sel_copy(g):
            if g >= 2:
                sp.wait("c_sel", g - 1)
                load(stg[g % 2][:, :, :], sel[:, 4 * g - 8:4 * g - 4, :], f"ld_sel{g % 2}")
            act.wait(f"ld_sel{g % 2}", 16 * (g // 2 + 1))
            act.do(lambda e: e.copy(selr[:, (4 * g + 8) % 16:(4 * g + 8) % 16 + 4, :], stg[g % 2][:, :, :]), "c_sel")

        done = {}

        def LX(c):
            if c >= 4:
                sp.wait(*done[("x1", 4 * (c - 4) + 3)])
            if c >= 1:
                x_load(c)
            if c >= 3:
                sp.wait("cT", c - 2)
            if c >= 1:
                c_load(c)

        def norm_stats(c, k, src):
            b = c % 2

            def stats(*i4):
                if c >= 1:
                    dve.wait(f"mv{k}", 4 * c)
                for i in i4:
                    dve.do(lambda e, i=i: e.bn_stats(bst[:, k, i, :], src[:, i, :]), f"bst{k}")

            def aggr():
                dve.wait(f"bst{k}", 4 * c + 4)
                if c >= 2:
                    dve.wait(f"rs{k}", c - 1)
                    dve.wait(f"nm_{k}", c - 1)
                for i in range(4):
                    dve.do(lambda e, i=i: e.bn_aggr(mv[b][:, k, i, :], bst[:, k, i, :]), f"mv{k}")
                pool.wait("c_nh", 1)
                pool.wait(f"mv{k}", 4 * c + 4)
                pool.do(lambda e: e.tensor_scalar(ve[b][:, k, :], mv[b][:, k, :, 1], EPS, None, ALU.add), f"ve{k}")
                pool.do(lambda e: e.tensor_scalar(ng[b][:, k, :], mv[b][:, k, :, 0], -1.0, None, ALU.mult), f"nm_{k}")
                pool.wait(f"ve{k}", c + 1)
                pool.do(lambda e: e.tensor_tensor(rs[b][:, k, :], ve[b][:, k, :], nhalf[:, :], ALU.pow), f"rs{k}")

            return [lambda: stats(0, 1), lambda: stats(2, 3), aggr]

        def norm_apply(c, k, dst, src, sem):
            b = c % 2
            pool.wait(f"rs{k}", c + 1)
            for i in range(4):
                pool.do(lambda e, i=i: e.tensor_scalar(dst[:, i, :], src[:, i, :], ng[b][:, k, i:i + 1], rs[b][:, k, i:i + 1],
                                                       ALU.add, ALU.mult), sem)

        def LN1(c):
            steps = norm_stats(c, 0, xin[c % 4])
            return [lambda: dve.wait(f"lx{c % 4}", 16 * (c // 4 + 1)) or steps[0]()] + steps[1:] + ([weights_prep] if c == 0 else [])

        def XH(c):
            if c >= 2:
                dve.wait("xT", c - 1)
            norm_apply(c, 0, xh[c % 2], xin[c % 4], "xh")
            if c == 0:
                clear(1)

        def XP(c):
            pool.wait("ld_v", n_ldv)
            pool.wait("xh", 4 * c + 4)
            for i in range(4):
                pool.do(lambda e, i=i: e.tensor_tensor(xin[c % 4][:, i, :], xin[c % 4][:, i, :], pbb[:, :], ALU.add), "xp")

        def XT(c):
            pe.wait("ld_id", 16)
            pe.wait("xh", 4 * c + 4)
            t, s = misc.take(pe)
            for i in range(4):
                pe.do(lambda e, i=i: e.transpose(t[:, i * 128:(i + 1) * 128], xh[c % 2][:, i, :], idf[:, :]),
                      "xT" if i == 3 else None)
            act.wait("xT", c + 1)
            act.wait("q", c)
            act.do(lambda e: e.copy(xTh[:, :], t[:, :]), "xTh")
            if c == 0:
                sel_copy(0)
                sel_copy(1)
            dve.wait("xTh", c + 1)
            dve.do(lambda e: e.tensor_tensor(xTl[:, :], t[:, :], xTh[:, :].bitcast(F), ALU.subtract), s)
            done[("xTl", c)] = (s, sems.count[s])

        def three(pe, out, w, xs, sem):
            (wh, wl), (xh_, xl) = w, xs
            pe.do(lambda e: e.matmul(out, wl, xh_, start=True, stop=False))
            pe.do(lambda e: e.matmul(out, wh, xh_, start=False, stop=False))
            pe.do(lambda e: e.matmul(out, wh, xl, start=False, stop=True), sem)


        def QP(c):
            pe.wait("c_lo", 3)
            pe.wait(*done[("xTl", c)])
            t, s = misc.take(pe)
            three(pe, t[:, :], (qwh[:, :], qwl[:, :]), (xTh[:, :], xTl[:, :]), "q")
            act.wait("c_qb", 1)
            act.wait("q", c + 1)
            act.wait("ql", c)
            act.do(lambda e: e.activation(qf[:, :], t[:, :], ACT.Identity, bias=cols[:, 0:1], scale=SCALE), s)
            done[("qf", c)] = (s, sems.count[s])

        def QH(c):
            dve.wait(*done[("qf", c)])
            dve.wait("qc", 4 * c)
            dve.do(lambda e: e.tensor_copy(qh[:, :], qf[:, :]), "qh")

        def QL(c):
            dve.wait("qh", c + 1)
            dve.do(lambda e: e.tensor_tensor(ql[:, :], qf[:, :], qh[:, :].bitcast(F), ALU.subtract), "ql")

        def CT(c):
            pe.wait("ld_id", 16)
            pe.wait(f"lc{c % 3}", 16 * (c // 3 + 1))
            t, s = misc.take(pe)
            for i in range(4):
                pe.do(lambda e, i=i: e.transpose(t[0:CD, i * CS:(i + 1) * CS], cin[c % 3][:, i, :], idf[0:CS, 0:CS]),
                      "cT" if i == 3 else None)
            act.wait("cT", c + 1)
            if c >= 2:
                act.wait("v", c - 1)
            act.do(lambda e: e.copy(cf[c % 2][:, :], t[0:CD, 0:KC]), s)
            done[("cf", c)] = (s, sems.count[s])

        def CH(c):
            dve.wait(*done[("cf", c)])
            dve.wait("k", c)
            dve.do(lambda e: e.tensor_copy(ch[:, :], cf[c % 2][:, :]), "ch")

        def CL(c):
            dve.wait("ch", c + 1)
            dve.do(lambda e: e.tensor_tensor(cl[:, :], cf[c % 2][:, :], ch[:, :].bitcast(F), ALU.subtract), "cl")

        def KP(c):
            pe.wait("cl", c + 1)
            t, s = misc.take(pe)
            three(pe, t[:, 0:KC], (kwh[:, :], kwl[:, :]), (ch[:, :], cl[:, :]), "k")
            act.wait("k", c + 1)
            act.wait("kl", c)
            act.do(lambda e: e.activation(kf[:, :], t[:, 0:KC], ACT.Identity, bias=cols[:, 1:2]), s)
            done[("kf", c)] = (s, sems.count[s])
            if c == 0:
                sel_copy(2)
                sel_copy(3)

        def KH(c):
            dve.wait(*done[("kf", c)])
            dve.wait("kc", 4 * c)
            dve.do(lambda e: e.tensor_copy(kh[:, :], kf[:, :]), "kh")

        def KL(c):
            dve.wait("kh", c + 1)
            dve.do(lambda e: e.tensor_tensor(kl[:, :], kf[:, :], kh[:, :].bitcast(F), ALU.subtract), "kl")

        def QC(c, g):
            pe.wait("c_sel", 4)
            pe.wait("ql", c + 1)
            t, s = misc.take(pe)
            pe.do(lambda e: e.matmul(t[:, :], selr[:, g, :], qh[:, :], start=True, stop=False))
            pe.do(lambda e: e.matmul(t[:, :], selr[:, 4 + g, :], ql[:, :], start=False, stop=True), "qc")
            q = act if g % 2 else dve
            q.wait("qc", 4 * c + g + 1)
            if c >= 2:
                q.wait("S", 16 * (c - 1))
                for p in (2 * c - 4, 2 * c - 3):
                    q.wait(f"qd{p % 2}", 64 * (p // 2 + 1))
            v = t[:, :].rearrange("p (i n) -> p i n", i=4)
            if g % 2:
                q.do(lambda e: e.copy(qc[c % 2][:, :, g, :], v), s)
            else:
                q.do(lambda e: e.tensor_copy(qc[c % 2][:, :, g, :], v), s)
            done[("qc", c, g)] = (s, sems.count[s])

        def KCOMB(c, g):
            pe.wait("c_sel", 2)
            pe.wait("kl", c + 1)
            t, s = misc.take(pe)
            pe.do(lambda e: e.matmul(t[:, 0:KC], selr[:, 8 + g, :], kh[:, :], start=True, stop=False))
            pe.do(lambda e: e.matmul(t[:, 0:KC], selr[:, 12 + g, :], kl[:, :], start=False, stop=True), "kc")
            act.wait("kc", 4 * c + g + 1)
            if c >= 2:
                act.wait("T", 16 * (c - 1))
                for p in (2 * c - 4, 2 * c - 3):
                    act.wait(f"kd{p % 2}", 64 * (p // 2 + 1))
            act.do(lambda e: e.activation(kc[c % 2][:, :, g, :], t[:, 0:KC].rearrange("p (i n) -> p i n", i=4), ACT.Identity,
                                          bias=cols[:, 4:5]), s)
            done[("kc", c, g)] = (s, sems.count[s])

        def VP(c):
            pe.wait("ld_v", n_ldv)
            t, s = misc.take(pe)
            for i in range(4):
                pe.do(lambda e, i=i: e.matmul(t[0:CS, i * 128:(i + 1) * 128], cf[c % 2][:, i * CS:(i + 1) * CS], vwf[:, :],
                                              start=True, stop=True), "v" if i == 3 else None)
            dve.wait("v", c + 1)
            dve.wait("ld_v", n_ldv)
            dve.wait("c_v9", 2)
            if c >= 2:
                dve.wait("Og", 16 * (c - 1))
            for i in range(4):
                dve.do(lambda e, i=i: e.tensor_tensor(v9[c % 2][:, i * H:(i + 1) * H, 0:8],
                                                      t[0:CS, i * 128:(i + 1) * 128].rearrange("p (h d) -> p h d", h=H),
                                                      vbb[:, :].rearrange("p (h d) -> p h d", h=H), ALU.add),
                       s if i == 3 else "v9")
            done[("v", c)] = (s, sems.count[s])

        def KD(p):
            c, i, s = p // 2, 2 * (p % 2), p % 2
            for g in range(4):
                sp.wait(*done[("kc", c, g)])
            sp.wait("c_kd", s + 1)
            if p >= 2:
                sp.wait("S", 8 * (p - 1))
            for j in range(4):
                load(kd[s][32 * j:32 * j + 32, :, :, j, :].rearrange("p i g m -> p (i g) m").bitcast(F),
                     kc[c % 2][32 * j:32 * j + 32, i:i + 2, :, :].rearrange("p i g m -> p (i g) m").bitcast(F), f"kd{s}")

        def QD(p):
            c, i, s = p // 2, 2 * (p % 2), p % 2
            for g in range(4):
                sp.wait(*done[("qc", c, g)])
            sp.wait("c_qd", s + 1)
            if p >= 2:
                sp.wait("T", 8 * (p - 1))
            for j in range(4):
                load(qd[s][32 * j:32 * j + 32, :, :, j, :].rearrange("p i g m -> p (i g) m").bitcast(F),
                     qc[c % 2][32 * j:32 * j + 32, i:i + 2, :, :].rearrange("p i g m -> p (i g) m").bitcast(F), f"qd{s}")

        def SC(b, g):
            c, i, p = b // 4, b % 4, b // 2
            pe.wait(*done[("qc", c, g)])
            pe.wait(f"kd{p % 2}", 64 * (p // 2 + 1))
            t, f = bS.take(pe)
            pe.do(lambda e: e.matmul(t[:, 0:KC], qc[c % 2][:, i, g, :], kd[p % 2][:, b % 2, g, :, :], start=True, stop=True), "S")
            dve.wait("S", 4 * b + g + 1)
            if b >= 2:
                dve.wait("mT", b - 1)
            dve.do(lambda e: e.tensor_reduce(mx[b % 2][:, 4 * g:4 * g + 4], t[:, 0:KC].rearrange("p (j m) -> p j m", j=4),
                                             AX.X, ALU.max, negate=True), f)
            done[("mx", b, g)] = (f, sems.count[f])

        def MT(b):
            p = b // 2
            for g in range(4):
                pe.wait(*done[("mx", b, g)])
            t, f = misc.take(pe)
            pe.do(lambda e: e.transpose(t[0:16, 0:128], mx[b % 2][:, :], idf[:, :]), "mT")
            act.wait("mT", b + 1)
            if b >= 2:
                act.wait(f"nm{b % 2}", 16 * (b // 2))
            act.do(lambda e: e.copy(nm[b % 2][:, :], t[0:16, 0:128]), f)
            sp.wait(f, sems.count[f])
            sp.wait(f"qd{p % 2}", 64 * (p // 2 + 1))
            load(qd[p % 2][24:25, b % 2, :, :, :].rearrange("p g j n -> p (g j) n").bitcast(F), nm[b % 2][:, :].bitcast(F), f"nm{b % 2}")

        def ST(b, g):
            c, i, p, k = b // 4, b % 4, b // 2, 4 * b + g
            pe.wait(f"nm{b % 2}", 16 * (b // 2 + 1))
            t, f = bT.take(pe)
            pe.do(lambda e: e.matmul(t[0:CS, :], kc[c % 2][:, i, g, :], qd[p % 2][:, b % 2, g, :, :], start=True, stop=True), "T")
            act.wait("T", k + 1)
            if k >= 4:
                act.wait("Og", k - 3)
            act.do(lambda e: e.activation(P[k % 4][:, :], t[0:CS, :], ACT.Exp), f)
            done[("p", b, g)] = (f, sems.count[f])

        def PV(b, g):
            c, i, k = b // 4, b % 4, 4 * b + g
            pe.wait(*done[("v", c)])
            pe.wait("c_o", 1)
            pe.wait(*done[("p", b, g)])
            if g == 0:
                PV.t, PV.f = bO.take(pe)
            t, f = PV.t, PV.f
            for j in range(4):
                pe.do(lambda e, j=j: e.matmul(t[32 * j:32 * j + 9, g * 128:(g + 1) * 128], v9[c % 2][:, i * H + 4 * g + j, :],
                                              P[k % 4][:, j * S:(j + 1) * S], start=True, stop=True),
                      "Og" if j == 3 else None)
            if g == 3:
                act.wait("Og", k + 1)
                if b >= 2:
                    act.wait("oX", b - 1)
                act.wait("c_z", 2)
                act.do(lambda e: e.copy(osb[b % 2][:, :, :], t[:, :]), f)
                done[("osb", b)] = (f, sems.count[f])

        def OT(b):
            pe.wait(*done[("osb", b)])
            t, f = misc.take(pe)
            for g in range(4):
                pe.do(lambda e, g=g: e.transpose(t[:, g * 128:(g + 1) * 128], osb[b % 2][:, g, :], idf[:, :]),
                      "oX" if g == 3 else None)
            v = t[:, :].rearrange("p (h r) -> p h r", r=32)
            dve.wait("oX", b + 1)
            if b >= 2:
                dve.wait(done[("on", b - 2)][0], done[("on", b - 2)][1])
            dve.do(lambda e: e.reciprocal(rd[b % 2][:, :], v[:, :, 8]), "rd")
            dve.wait("rd", b + 1)
            if b >= 2:
                dve.wait("onT", b - 1)
            dve.do(lambda e: e.tensor_tensor(on[b % 2][:, :].rearrange("p (h d) -> p h d", d=8), v[:, :, 0:8],
                                             rd[b % 2][:, :].unsqueeze(2).to_broadcast([128, 16, 8]), ALU.mult), f)
            done[("on", b)] = (f, sems.count[f])

        def ONT(b):
            pe.wait(*done[("on", b)])
            t, f = misc.take(pe)
            pe.do(lambda e: e.transpose(t[:, 0:128], on[b % 2][:, :], idf[:, :]), "onT")
            act.wait("onT", b + 1)
            if b >= 2:
                act.wait("pr", b - 1)
            act.do(lambda e: e.copy(oT[b % 2][:, :], t[:, 0:128]), f)
            done[("oT", b)] = (f, sems.count[f])

        def PR(b):
            c, i = b // 4, b % 4
            pe.wait(*done[("oT", b)])
            t, f = misc.take(pe)
            pe.do(lambda e: e.matmul(t[:, 0:128], oT[b % 2][:, :], pwf[:, :], start=True, stop=True), "pr")
            dve.wait("pr", b + 1)
            dve.wait("xp", 4 * c + 4)
            if c >= 3:
                dve.wait("xr", 4 * (c - 2))
            dve.do(lambda e: e.tensor_tensor(x1[c % 3][:, i, :], t[:, 0:128], xin[c % 4][:, i, :], ALU.add), f)
            done[("x1", b)] = (f, sems.count[f])

        def N2(c):
            steps = norm_stats(c, 1, x1[c % 3])

            def first():
                for b in range(4 * c, 4 * c + 4):
                    dve.wait(*done[("x1", b)])
                steps[0]()

            def apply():
                pool.wait("c_lo", 3)
                if c >= 2:
                    pool.wait("xr", 4 * (c - 1))
                    pool.wait("bst2", 4 * (c - 1))
                norm_apply(c, 1, hh[c % 2], x1[c % 3], "hh")

            return [first] + steps[1:] + [None] * 5 + [apply]

        def XR(c):
            pool.wait("hh", 4 * c + 4)
            if c >= 2:
                pool.wait(f"sx{c % 2}", 16 * (c // 2))
            for i in range(4):
                pool.do(lambda e, i=i: e.tensor_tensor(xr[c % 2][:, i, :], x1[c % 3][:, i, :], hh[c % 2][:, i, :], ALU.add), "xr")

        def XS(c):
            sp.wait("xr", 4 * c + 4)
            load(xres[c], xr[c % 2][:, :, :].rearrange("p a b -> p (a b)"), f"sx{c % 2}")

        def N3(c):
            steps = norm_stats(c, 2, hh[c % 2])

            def apply():
                pool.wait("c_sel", 4)
                if c >= 2:
                    pool.wait("zT", c - 1)
                norm_apply(c, 2, zz[c % 2], hh[c % 2], "zz")

            return [lambda: dve.wait("hh", 4 * c + 4) or steps[0]()] + steps[1:] + [None] * 5 + [apply]

        def ZT(c):
            pe.wait("zz", 4 * c + 4)
            t, f = misc.take(pe)
            for i in range(4):
                pe.do(lambda e, i=i: e.transpose(t[:, i * 128:(i + 1) * 128], zz[c % 2][:, i, :], idf[:, :]),
                      "zT" if i == 3 else None)
            act.wait("zT", c + 1)
            act.wait("ld_v", n_ldv)
            act.do(lambda e: e.activation(xnT[:, c * TC:(c + 1) * TC], t[:, :], ACT.Identity, bias=cols[:, 3:4],
                                          scale=cols[:, 2:3]), f)
            done[("xn", c)] = (f, sems.count[f])

        def ZH(c):
            dve.wait(*done[("xn", c)])
            dve.wait("rt", c)
            dve.do(lambda e: e.tensor_copy(zh[:, :], xnT[:, c * TC:(c + 1) * TC]), "zh")

        def ZL(c):
            dve.wait("zh", c + 1)
            dve.do(lambda e: e.tensor_tensor(zl[:, :], xnT[:, c * TC:(c + 1) * TC], zh[:, :].bitcast(F), ALU.subtract), "zl")

        def RT(c):
            pe.wait("zl", c + 1)
            t, f = misc.take(pe)
            three(pe, t[:, :], (rwh[:, :], rwl[:, :]), (zh[:, :], zl[:, :]), "rt")
            act.wait("rt", c + 1)
            act.wait("lT", c)
            act.do(lambda e: e.copy(lg[:, :], t[0:8, :]), f)
            done[("lg", c)] = (f, sems.count[f])

        def LT(c):
            b = c % 2
            pe.wait(*done[("lg", c)])
            t, f = misc.take(pe)
            for i in range(4):
                pe.do(lambda e, i=i: e.transpose(t[:, i * 8:(i + 1) * 8], lg[:, i * 128:(i + 1) * 128], idf[0:8, 0:8]),
                      "lT" if i == 3 else None)
            v = t[:, 0:32].rearrange("p (i e) -> p i e", e=8)
            dve.wait("lT", c + 1)
            dve.do(lambda e: e.tensor_reduce(s4[b][:, 0, :], v, AX.X, ALU.max), "r1")
            done[("lgt", c)] = (v, f)

        def LS(c):
            b = c % 2
            v, f = done[("lgt", c)]
            dve.wait("r1", c + 1)
            dve.do(lambda e: e.tensor_tensor(sm[b][:, 0, :, :], v, s4[b][:, 0, :].unsqueeze(2).to_broadcast([128, 4, 8]),
                                             ALU.subtract), f)
            done[("ls", c)] = (f, sems.count[f])

        def LE(c):
            b = c % 2
            act.wait(*done[("ls", c)])
            act.do(lambda e: e.activation(sm[b][:, 1, :, :], sm[b][:, 0, :, :], ACT.Exp, scale=1.0 / TEMP), "r2")

        def TOP(c):
            b = c % 2
            s_, r_ = sm[b], s4[b]

            def total():
                dve.wait("r2", c + 1)
                dve.do(lambda e: e.tensor_reduce(r_[:, 1, :], s_[:, 1, :, :], AX.X, ALU.add), "r3")

            def inverse():
                dve.wait("r3", c + 1)
                dve.do(lambda e: e.reciprocal(r_[:, 2, :], r_[:, 1, :]), "r4")

            def probs():
                dve.wait("r4", c + 1)
                dve.do(lambda e: e.tensor_tensor(s_[:, 2, :, :], s_[:, 1, :, :],
                                                 r_[:, 2, :].unsqueeze(2).to_broadcast([128, 4, 8]), ALU.mult), "r5")

            def sort(*i4):
                dve.wait("r5", c + 1)
                for i in i4:
                    dve.do(lambda e, i=i: e.max(m8[b][:, i, :], s_[:, 2, i, :]), "r6")

            def index(*i4):
                dve.wait("r6", 4 * c + 4)
                for i in i4:
                    dve.do(lambda e, i=i: e.max_index(i8[b][:, i, :], m8[b][:, i, :], s_[:, 2, i, :]), "r7")

            def floats():
                dve.wait("r7", 4 * c + 4)
                dve.do(lambda e: e.tensor_copy(if8[b][:, :, :], i8[b][:, :, :]), "r8")

            def equal():
                dve.wait("r8", c + 1)
                for k in range(2):
                    dve.do(lambda e, k=k: e.tensor_tensor(s_[:, 3 * k, :, :], iot[:, :, :],
                                                          if8[b][:, :, k].unsqueeze(2).to_broadcast([128, 4, 8]),
                                                          ALU.is_equal), "r9")

            def either():
                dve.wait("r9", 2 * c + 2)
                dve.do(lambda e: e.tensor_tensor(s_[:, 0, :, :], s_[:, 0, :, :], s_[:, 3, :, :], ALU.add), "r10")

            def weights():
                dve.wait("r10", c + 1)
                if c >= 2:
                    dve.wait("wT", c - 1)
                dve.do(lambda e: e.tensor_tensor(wd[b][:, :, :], s_[:, 0, :, :], s_[:, 2, :, :], ALU.mult), "wd")

            return [total, inverse, probs, lambda: sort(0, 1), lambda: sort(2, 3), lambda: index(0, 1), lambda: index(2, 3), floats, equal, either, weights]

        def WT(c):
            b = c % 2
            pe.wait("wd", c + 1)
            t, f = misc.take(pe)
            pe.do(lambda e: e.transpose(t[0:32, 0:128], wd[b][:, :, :].rearrange("p a b -> p (a b)"), idf[:, :]), "wT")
            act.wait("wT", c + 1)
            if c >= 2:
                act.wait(f"sw{b}", 16 * (c // 2))
            act.do(lambda e: e.copy(wts[b][:, :], t[0:32, 0:128]), f)
            sp.wait(f, sems.count[f])
            load(wsc[c], wts[b][:, :], f"sw{b}")

        def at(c, *fns):
            return [lambda fn=fn: fn(c) for fn in fns] if 0 <= c < NC else []

        def front(c0, i):
            c, n = c0 + 1, c0 + 2
            if i == 0:
                return at(c, CT, CH, CL, XT, XP)
            if i == 1:
                return at(c, KP, QP, KH) + at(n, LX) + at(c, KL, QH, QL) + [None]
            two = lambda *gs: [(lambda g=g: KCOMB(c, g)) if k == "k" else (lambda g=g: QC(c, g)) for k, g in gs] if 0 <= c < NC else []
            if i == 2:
                return two(("k", 0), ("k", 1), ("k", 2), ("k", 3), ("q", 0), ("q", 1)) + (LN1(n) if 0 <= n < NC else [])
            return two(("q", 2), ("q", 3)) + at(c, VP) + at(n, XH)

        gap = lambda n: [None] * n

        def norms(c):
            return N2(c) + gap(9) + N3(c) + at(c, XR) + gap(12) + at(c, XS, ZT) + gap(4) + at(c, ZH, ZL)

        def router(c):
            return (at(c, RT) + gap(6) + at(c, LT) + [None] + at(c, LS) + gap(2) + at(c, LE) + gap(3) + TOP(c)
                    + gap(8) + at(c, WT))

        wraw = [xh]
        W2v = W2.rearrange("e (k p) d -> e p k d", p=128)

        def WL(e_):
            s = e_ % 2
            if e_ >= 2:
                sp.wait("wlo", 2 * (e_ - 1))
            if e_ == 0:
                sp.wait("xT", NC)
            load(flat(wraw[s][0]), W1[e_], f"wr{s}")
            load(flat(wraw[s][1]).rearrange("p (k d) -> p k d", k=4), W2v[e_], f"wr{s}")

        def flat(t):
            return t[:, :, :].rearrange("p a b -> p (a b)") if len(t.shape) == 3 else t[:, :]

        def WS(e_, w):
            s = e_ % 2
            pool.wait(f"wr{s}", 32 * (e_ // 2 + 1))
            for k in range(2):
                pool.do(lambda e, k=k: e.tensor_copy(w(2 * k, e_), flat(wraw[s][k])), "whi")
            pool.wait("whi", 2 * e_ + 2)
            for k in range(2):
                pool.do(lambda e, k=k: e.tensor_tensor(w(2 * k + 1, e_), flat(wraw[s][k]), w(2 * k, e_).bitcast(F),
                                                       ALU.subtract), "wlo")

        def GP(c, hi, lo):
            dve.wait(*done[("xn", c)])
            dve.do(lambda e: e.tensor_copy(hi[:, :], xnT[:, c * TC:(c + 1) * TC]), "gh")
            dve.wait("gh", c + 1)
            dve.do(lambda e: e.tensor_tensor(lo[:, :], xnT[:, c * TC:(c + 1) * TC], hi[:, :].bitcast(F), ALU.subtract), "gl")

        def first_weights():
            pool.wait("qc", 4 * NC)
            pool.wait("kc", 4 * NC)
            WS(0, lambda kind, e_: selr[:, 4 * kind:4 * kind + 4, :].rearrange("p a b -> p (a b)"))
            dve.wait("q", NC)
            GP(0, xTh, xTl)

        tails = [[], []]

        def go():
            for steps_ in tails:
                f_ = steps_.pop(0) if steps_ else None
                if f_:
                    f_()

        ok = lambda b: 0 <= b < NB
        for t in range(-8, NB + 4):
            c0, i = divmod(t, 4)
            if i == 1 and 0 <= c0 - 2 < NC:
                tails[0] += norms(c0 - 2)
            if i == 1 and 0 <= c0 - 3 < NC:
                tails[1] += router(c0 - 3)
            if t == NB - 2:
                WL(0)
            if t == NB:
                first_weights()
            near = front(c0, i)
            steps = []
            if t % 2 == 1 and ok(t + 1):
                KD((t + 1) // 2)
            if t % 2 == 0 and ok(t):
                steps.append(lambda: QD(t // 2))
            u, v = t - 2, t - 3
            kinds = {"SC": (t, lambda g: SC(t, g)), "ST": (u, lambda g: ST(u, g)), "Pv": (v, lambda g: PV(v, g)),
                     "Pu": (u, lambda g: PV(u, g)), "ON": (t - 4, lambda g: ONT(t - 4)), "MT": (t - 1, lambda g: MT(t - 1)),
                     "PR": (t - 4, lambda g: PR(t - 4)), "OT": (v, lambda g: OT(v))}
            for w in ORDER.split():
                b_, fn = kinds[w[:2]]
                if ok(b_):
                    steps.append(lambda fn=fn, w=w: fn(int(w[2:] or 0)))
            n = max(len(steps), 1)
            fed = 0
            for k in range(n):
                if k < len(steps):
                    steps[k]()
                while near and fed < len(near) * (k + 1) // n:
                    f_ = near[fed]
                    fed += 1
                    if f_:
                        f_()
                go()
            for f_ in near[fed:]:
                if f_:
                    f_()
        tails[1] += gap(max(len(tails[0]) - len(tails[1]), 0) + 3) + router(NC - 2)
        tails[0] += norms(NC - 1)
        tails[1] += gap(max(len(tails[0]) - len(tails[1]), 0) + 5) + router(NC - 1)
        misc.turn = [2]

        endA = {k: v for k, v in sems.count.items() if v}
        sa.close()

        sb_ = ExitStack()
        nb = [0]

        def Bt(shape, dt=F, n=1):
            nb[0] += 1
            ts = [sbt(sb_, f"b{nb[0]}_{i}", shape, dt) for i in range(n)]
            return ts[0] if n == 1 else ts

        wx = Bt([128, E - 1, 4, 512], R)
        wraw.append([Bt([128, 512]), Bt([128, 512])])
        gh, gl = [xTh, Bt([128, TC], R)], [xTl, Bt([128, TC], R)]
        sf, sh, sl = Bt([128, TC], F, 3), Bt([128, TC], R, 6), Bt([128, TC], R, 6)
        wb = Bt([128, TC], F, 4)
        ty = Bt([128, TC], F, 2)
        acc = Bt([128, TC], F, 2)
        xo = Bt([128, TC], F, 2)
        oo = Bt([128, TC], F, 2)
        bH = Banks("bH", bS.tiles + bT.tiles)
        bY, bF = InOrder("yw", [misc.tiles[0], bO.tiles[0]]), InOrder("oo", [misc.tiles[1]])

        for q in (act, dve, pool, sp):
            for k, v in endA.items():
                q.wait(k, v)
        for b_ in (bS, bT):
            for s_ in range(2):
                b_.free(pe, s_)

        def W(kind, e_):
            if e_ == 0:
                return selr[:, 4 * kind:4 * kind + 4, :].rearrange("p a b -> p (a b)")
            return wx[:, e_ - 1, kind, :]

        def WB(u):
            (c, e_), s = units[u], u % 4
            if u >= 4:
                sp.wait("yw", u - 3)
            sp.wait(f"sw{c % 2}", 16 * (c // 2 + 1))
            src = wsc[c].rearrange("(t e) n -> e t n", t=4)[e_].partition_broadcast(128)
            load(wb[s][:, :].rearrange("p (t n) -> p t n", t=4), src, f"wb{s}")

        units = [(c, e_) for e_ in range(E) for c in range(2)] + [(c, e_) for c in range(2, NC) for e_ in range(E)]
        last = {c: units.index((c, E - 1)) for c in range(NC)}
        accs = {}

        def M1(u, f):
            (c, e_), k = units[u], 4 * u + f
            pe.wait("wlo", 2 * e_ + 2)
            pe.wait("gl", c + 1)
            t, s = bH.take(pe)
            fs = slice(f * 128, (f + 1) * 128)
            three(pe, t[:, :], (W(0, e_)[:, fs], W(1, e_)[:, fs]), (gh[c % 2][:, :], gl[c % 2][:, :]), "M1")
            act.wait("M1", k + 1)
            if k >= 3:
                act.wait("sl", k - 2)
            act.do(lambda e: e.activation(sf[k % 3][:, :], t[:, :], ACT.Silu), "sf")
            if k >= 6:
                act.wait("M2", k - 5)
            act.do(lambda e: e.activation(sh[k % 6][:, :], t[:, :], ACT.Silu), s)
            dve.wait("sf", k + 1)
            dve.wait(s, sems.count[s])
            if k >= 6:
                dve.wait("M2", k - 5)
            dve.do(lambda e: e.tensor_tensor(sl[k % 6][:, :], sf[k % 3][:, :], sh[k % 6][:, :].bitcast(F), ALU.subtract), "sl")

        def M2(u, f):
            (c, e_), k = units[u], 4 * u + f
            pe.wait("sl", k + 1)
            if k == 0:
                misc.free(pe, 0)
                misc.free(pe, 1)
                bO.free(pe, 0)
            if f == 0:
                M2.t, _ = bY.take(pe)
            t = M2.t
            fs = slice(f * 128, (f + 1) * 128)
            pe.do(lambda e: e.matmul(t[:, :], W(3, e_)[:, fs], sh[k % 6][:, :], start=(f == 0), stop=False))
            pe.do(lambda e: e.matmul(t[:, :], W(2, e_)[:, fs], sh[k % 6][:, :], start=False, stop=False))
            pe.do(lambda e: e.matmul(t[:, :], W(2, e_)[:, fs], sl[k % 6][:, :], start=False, stop=(f == 3)), "M2")

        def YW(u):
            (c, e_), s = units[u], u % 4
            t = M2.t
            dve.wait("M2", 4 * u + 4)
            dve.wait(f"wb{s}", 16 * (u // 4 + 1))
            if e_ == 0:
                if c >= 2:
                    dve.wait("fT", c - 1)
                dve.do(lambda e: e.tensor_tensor(acc[c % 2][:, :], t[:, :], wb[s][:, :], ALU.mult), "yw")
            else:
                dve.do(lambda e: e.tensor_tensor(ty[u % 2][:, :], t[:, :], wb[s][:, :], ALU.mult), "yw")
            dve.wait("yw", u + 1)
            if e_:
                if e_ > 1:
                    dve.wait("ac", accs[c])
                dve.do(lambda e: e.tensor_tensor(acc[c % 2][:, :], acc[c % 2][:, :], ty[u % 2][:, :], ALU.add), "ac")
                accs[c] = sems.count["ac"]

        def XO(c):
            s = c % 2
            if c >= 2:
                sp.wait("oo", c - 1)
            sp.wait(f"sx{s}", 16 * (c // 2 + 1))
            load(xo[s][:, :], xres[c], f"xo{s}")

        def FIN(c):
            s = c % 2
            pe.wait("ac", accs[c])
            t, f = bF.take(pe)
            for i in range(4):
                pe.do(lambda e, i=i: e.transpose(t[:, i * 128:(i + 1) * 128], acc[s][:, i * 128:(i + 1) * 128], idf[:, :]),
                      "fT" if i == 3 else None)
            dve.wait("fT", c + 1)
            dve.wait(f"xo{s}", 16 * (c // 2 + 1))
            if c >= 2:
                dve.wait(f"so{s}", 16 * (c // 2))
            dve.do(lambda e: e.tensor_tensor(oo[s][:, :], t[:, :], xo[s][:, :], ALU.add), "oo")
            sp.wait("oo", c + 1)
            load(out[4 * c:4 * c + 4].rearrange("b n d -> n b d"), oo[s][:, :].rearrange("p (b d) -> p b d", b=4), f"so{s}")

        WL(1)
        WB(0)
        WB(1)
        GP(1, gh[1], gl[1])
        WS(1, W)
        NU = NC * E
        LAG = 3
        for k in range(4 * NU + LAG + 1):
            u, f = divmod(k, 4)
            if u < NU:
                c, e_ = units[u]
                if f == 0:
                    if u % 2 == 0 and u < 2 * E - 4:
                        WL(u // 2 + 2)
                        WS(u // 2 + 2, W)
                    if u + 2 < NU:
                        WB(u + 2)
                    if e_ == 4:
                        XO(c)
                M1(u, f)
                n = c + 1
                if c >= 1 and n < NC and ((n > 2 and f == 3 and e_ == 3) or (n == 2 and f == 0 and e_ == E - 1)):
                    dve.wait("M1", 4 * last[n - 2] + 4)
                    GP(n, gh[n % 2], gl[n % 2])
            k2 = k - LAG
            if 0 <= k2 < 4 * NU:
                u2, f2 = divmod(k2, 4)
                M2(u2, f2)
                if f2 == 3:
                    YW(u2)
            for c in range(NC):
                if k == 4 * last[c] + 10:
                    FIN(c)
            go()
        FIN(NC - 1)
        for s in range(2):
            sp.wait(f"so{s}", 16 * (NC // 2))
            sp.wait(f"sx{s}", 16 * (NC // 2))
            sp.wait(f"sw{s}", 16 * (NC // 2))

        block = st.enter_context(nc.Block())

        @block.sync
        def _(e):
            sp.emit(e)

        @block.tensor
        def _(e):
            pe.emit(e)

        @block.scalar
        def _(e):
            act.emit(e)

        @block.vector
        def _(e):
            dve.emit(e)

        @block.gpsimd
        def _(e):
            pool.emit(e)

        sb_.close()


def _selectors():
    import numpy as np
    sel = np.zeros((128, 16, 128), np.float32)
    for kind, parts in enumerate(((0, 2), (1,), (0, 1), (2,))):
        for g in range(4):
            for j in range(4):
                for d in range(HD):
                    for p in parts:
                        sel[(4 * g + j) * HD + d, 4 * kind + g, 32 * j + 8 * p + d] = 1.0
    return sel


def kernel(**inputs):
    import numpy as np
    import concourse.bacc as bacc
    from concourse.bass_utils import run_bass_kernel_spmd

    i = {k: np.asarray(v) for k, v in inputs.items()}
    col = lambda a: a.reshape(128, 1)
    rows = lambda a, n: np.broadcast_to(a.reshape(1, 128), (n, 128))
    one24 = np.zeros((128, 1), np.float32)
    one24[24] = 1.0
    iota = np.broadcast_to(np.arange(8, dtype=np.float32), (128, 4, 8))
    args = [
        ("x", i["x"]), ("ctx", i["ctx_768"]), ("qw", i["L0_xattn_q_w"]), ("qb", col(i["L0_xattn_q_b"])),
        ("kw", i["L0_xattn_kv_w"][:, 0:128]), ("kb", col(i["L0_xattn_kv_b"][0:128])),
        ("vw", i["L0_xattn_kv_w"][:, 128:256]), ("vb", rows(i["L0_xattn_kv_b"][128:256], CS)),
        ("pw", i["L0_xattn_proj_w"]), ("pb", rows(i["L0_xattn_proj_b"], 128)),
        ("gam", col(i["L0_ffn_gamma"])), ("bet", col(i["L0_ffn_beta"])), ("rwT", i["L0_ffn_router_w"].T),
        ("W1", i["L0_ffn_W1"]), ("W2", i["L0_ffn_W2"]), ("ident", np.eye(128, dtype=np.float32)),
        ("sel", _selectors()), ("one24", one24), ("iota", iota),
    ]
    nc = bacc.Bacc("TRN2", target_bir_lowering=False, num_devices=1)
    arrays, aps = {}, []
    for name, a in args:
        a = np.ascontiguousarray(a)
        arrays[f"in_{name}"] = a
        aps.append(nc.dram_tensor(f"in_{name}", a.shape, mybir.dt.from_np(a.dtype), kind="ExternalInput").ap())
    o = nc.dram_tensor("out_0", (NB, S, D), F, kind="ExternalOutput").ap()
    xattn_moe(nc, *aps, o)
    r = run_bass_kernel_spmd(nc, [arrays], core_ids=[0])
    return r.results[0]["out_0"]
```
